# Optimizing a Trainium2 kernel written in Bass

```python
import numpy as np
import jax
import jax.numpy as jnp

def _softmax(x, axis=-1):
    return jax.nn.softmax(x, axis=axis)

def _gelu(x):
    return jax.nn.gelu(x, approximate=True)

def _silu(x):
    return jax.nn.silu(x)

def _sigmoid(x):
    return jax.nn.sigmoid(x)

def _layernorm(x, axis=-1, eps=1e-05):
    m = jnp.mean(x, axis=axis, keepdims=True)
    v = jnp.var(x, axis=axis, keepdims=True)
    return (x - m) / jnp.sqrt(v + eps)

def _scatter_add(tgt, idx, src, axis=0):
    return tgt.at[idx].add(src)

def _segment_sum(src, seg, n):
    return jax.ops.segment_sum(src, seg, n)
kernel_name = 'mk_adaln_d1_jaxref_r8_6120d9'

def setup_inputs(seed: int=0):
    np.random.seed(seed)
    _w = jnp.asarray

    def _L0_attn_setup():
        import jax, jax.numpy as jnp
        import numpy as np
        import math
        D_MODEL = 128
        N_HEADS = 16
        D_K = D_MODEL // N_HEADS
        MAX_REL = 128

        def _rel_bias_matrix(rel_bias, seq_len):
            pos = jnp.arange(seq_len)
            rel = pos[:, None] - pos[None, :]
            idx = jnp.clip(rel, -MAX_REL, MAX_REL) + MAX_REL
            return rel_bias[:, idx]
        key = jax.random.key(seed)
        ks = jax.random.split(key, 10)
        B, S = (2, 256)
        std = 1.0 / math.sqrt(D_MODEL)
        inp = {'x': jax.random.normal(ks[0], (B, S, D_MODEL), dtype=jnp.float32), 'Wq': jax.random.normal(ks[1], (D_MODEL, D_MODEL), dtype=jnp.float32) * std, 'bq': jnp.zeros((D_MODEL,), dtype=jnp.float32), 'Wk': jax.random.normal(ks[2], (D_MODEL, D_MODEL), dtype=jnp.float32) * std, 'bk': jnp.zeros((D_MODEL,), dtype=jnp.float32), 'Wv': jax.random.normal(ks[3], (D_MODEL, D_MODEL), dtype=jnp.float32) * std, 'bv': jnp.zeros((D_MODEL,), dtype=jnp.float32), 'Wo': jax.random.normal(ks[4], (D_MODEL, D_MODEL), dtype=jnp.float32) * std, 'bo': jnp.zeros((D_MODEL,), dtype=jnp.float32), 'rel_bias': jax.random.normal(ks[5], (N_HEADS, 2 * MAX_REL + 1), dtype=jnp.float32) * 0.02}
        return inp
    _L0_attn_in = _L0_attn_setup()

    def _L0_ffn_setup():
        import jax, jax.numpy as jnp
        import numpy as np
        B, S, D, H, E = (4, 256, 128, 512, 8)
        EPS = 1e-12

        def _wn(v, g):
            n = jnp.sqrt(jnp.sum(v * v, axis=-1, keepdims=True))
            return v / jnp.maximum(n, EPS) * g[:, None]
        key = jax.random.key(seed)
        ks = jax.random.split(key, 8)
        return {'x': jax.random.normal(ks[0], (B, S, D), dtype=jnp.float32), 'gate_v': jax.random.normal(ks[1], (E, D), dtype=jnp.float32), 'gate_g': jnp.ones((E,), dtype=jnp.float32), 'gate_b': jnp.zeros((E,), dtype=jnp.float32), 'w1_v': jax.random.normal(ks[2], (E, H, D), dtype=jnp.float32), 'w1_g': jnp.ones((E, H), dtype=jnp.float32), 'b1': jnp.zeros((E, H), dtype=jnp.float32), 'w2_v': jax.random.normal(ks[3], (E, D, H), dtype=jnp.float32), 'w2_g': jnp.ones((E, D), dtype=jnp.float32), 'b2': jnp.zeros((E, D), dtype=jnp.float32)}
    _L0_ffn_in = _L0_ffn_setup()
    _L0_c = _w((lambda *s: np.random.randn(*s).astype(np.float32) * 0.05)(8, 128))
    _L0_wmod = _w((lambda *s: np.random.randn(*s).astype(np.float32) * 0.05)(128, 6 * 128) * 128 ** (-0.5))
    _d = {'L0_attn_x': _L0_attn_in['x'], 'L0_attn_Wq': _L0_attn_in['Wq'], 'L0_attn_bq': _L0_attn_in['bq'], 'L0_attn_Wk': _L0_attn_in['Wk'], 'L0_attn_bk': _L0_attn_in['bk'], 'L0_attn_Wv': _L0_attn_in['Wv'], 'L0_attn_bv': _L0_attn_in['bv'], 'L0_attn_Wo': _L0_attn_in['Wo'], 'L0_attn_bo': _L0_attn_in['bo'], 'L0_attn_rel_bias': _L0_attn_in['rel_bias'], 'L0_ffn_gate_v': _L0_ffn_in['gate_v'], 'L0_ffn_gate_g': _L0_ffn_in['gate_g'], 'L0_ffn_gate_b': _L0_ffn_in['gate_b'], 'L0_ffn_w1_v': _L0_ffn_in['w1_v'], 'L0_ffn_w1_g': _L0_ffn_in['w1_g'], 'L0_ffn_b1': _L0_ffn_in['b1'], 'L0_ffn_w2_v': _L0_ffn_in['w2_v'], 'L0_ffn_w2_g': _L0_ffn_in['w2_g'], 'L0_ffn_b2': _L0_ffn_in['b2'], 'L0_c': _L0_c, 'L0_wmod': _L0_wmod}
    _x0 = _d['L0_attn_x']
    _d['L0_attn_x'] = jax.random.normal(jax.random.fold_in(jax.random.key(seed), 1), (8, 256, 128), dtype=_x0.dtype)
    del _x0
    return _d

def reference(L0_attn_x, L0_attn_Wq, L0_attn_bq, L0_attn_Wk, L0_attn_bk, L0_attn_Wv, L0_attn_bv, L0_attn_Wo, L0_attn_bo, L0_attn_rel_bias, L0_ffn_gate_v, L0_ffn_gate_g, L0_ffn_gate_b, L0_ffn_w1_v, L0_ffn_w1_g, L0_ffn_b1, L0_ffn_w2_v, L0_ffn_w2_g, L0_ffn_b2, L0_c, L0_wmod):

    def _L0_attn_ref(x, Wq, bq, Wk, bk, Wv, bv, Wo, bo, rel_bias):
        import jax, jax.numpy as jnp
        import numpy as np
        import math
        D_MODEL = 128
        N_HEADS = 16
        D_K = D_MODEL // N_HEADS
        MAX_REL = 128

        def _rel_bias_matrix(rel_bias, seq_len):
            pos = jnp.arange(seq_len)
            rel = pos[:, None] - pos[None, :]
            idx = jnp.clip(rel, -MAX_REL, MAX_REL) + MAX_REL
            return rel_bias[:, idx]
        B, S, _ = x.shape

        def proj(W, b):
            y = x @ W.T + b
            return y.reshape(B, S, N_HEADS, D_K).transpose(0, 2, 1, 3)
        Q, K, V = (proj(Wq, bq), proj(Wk, bk), proj(Wv, bv))
        scores = jnp.einsum('bhqd,bhkd->bhqk', Q, K) / math.sqrt(D_K)
        scores = scores + _rel_bias_matrix(rel_bias, S)[None]
        attn = jax.nn.softmax(scores, axis=-1)
        out = jnp.einsum('bhqk,bhkd->bhqd', attn, V)
        out = out.transpose(0, 2, 1, 3).reshape(B, S, D_MODEL)
        return out @ Wo.T + bo

    def _L0_ffn_ref(x, gate_v, gate_g, gate_b, w1_v, w1_g, b1, w2_v, w2_g, b2):
        import jax, jax.numpy as jnp
        import numpy as np
        B, S, D, H, E = (4, 256, 128, 512, 8)
        EPS = 1e-12

        def _wn(v, g):
            n = jnp.sqrt(jnp.sum(v * v, axis=-1, keepdims=True))
            return v / jnp.maximum(n, EPS) * g[:, None]
        b, s, d = x.shape
        xf = x.reshape(-1, d)
        gw = _wn(gate_v, gate_g)
        gates = jax.nn.softmax(xf @ gw.T + gate_b, axis=-1)
        top_k = min(2, E)
        _, top_idx = jax.lax.top_k(gates, top_k)
        out = jnp.zeros_like(xf)
        for i in range(E):
            mask = jnp.any(top_idx == i, axis=1).astype(xf.dtype)[:, None]
            xm = xf * mask
            W1 = _wn(w1_v[i], w1_g[i])
            h = xm @ W1.T + b1[i]
            h = h * jax.nn.sigmoid(h)
            W2 = _wn(w2_v[i], w2_g[i])
            out = out + mask * (h @ W2.T + b2[i])
        return out.reshape(b, s, d)
    x = L0_attn_x
    mod = (_silu(L0_c) @ L0_wmod).reshape(L0_c.shape[0], 6, 1, -1)
    sa, ca, ga, sb, cb, gb = (mod[:, 0], mod[:, 1], mod[:, 2], mod[:, 3], mod[:, 4], mod[:, 5])
    ga = (2 * (ga >= 0) - 1) * jnp.maximum(jnp.abs(ga), 0.25)
    gb = (2 * (gb >= 0) - 1) * jnp.maximum(jnp.abs(gb), 0.25)
    h = _layernorm(x, axis=-1) * (1 + ca) + sa
    x = x + ga * _L0_attn_ref(h, L0_attn_Wq, L0_attn_bq, L0_attn_Wk, L0_attn_bk, L0_attn_Wv, L0_attn_bv, L0_attn_Wo, L0_attn_bo, L0_attn_rel_bias)
    h = _layernorm(x, axis=-1) * (1 + cb) + sb
    x = x + gb * _L0_ffn_ref(h, L0_ffn_gate_v, L0_ffn_gate_g, L0_ffn_gate_b, L0_ffn_w1_v, L0_ffn_w1_g, L0_ffn_b1, L0_ffn_w2_v, L0_ffn_w2_g, L0_ffn_b2)
    return x

_drawn_inputs = setup_inputs


def setup_inputs(seed=0):
    import zlib

    import numpy as np

    out = dict(_drawn_inputs(seed))
    spreads = {'L0_attn_bq': (0.0, 0.463),
     'L0_attn_bk': (0.0, 2.0),
     'L0_attn_bv': (0.0, 0.1),
     'L0_attn_bo': (0.0, 0.1),
     'L0_ffn_gate_g': (1.0, 0.2),
     'L0_ffn_gate_b': (0.0, 0.1),
     'L0_ffn_w1_g': (1.0, 0.2),
     'L0_ffn_b1': (0.0, 0.365),
     'L0_ffn_w2_g': (1.0, 0.2),
     'L0_ffn_b2': (0.0, 0.1)}
    factors = {'L0_attn_rel_bias': 27.344}
    for name, (base, spread) in spreads.items():
        noise = np.random.default_rng([zlib.crc32(name.encode()), seed]).standard_normal(out[name].shape)
        drawn = base * np.exp(spread * noise) if base else spread * noise
        out[name] = jnp.asarray(drawn.astype(out[name].dtype))
    for name, factor in factors.items():
        out[name] = (out[name] * factor).astype(out[name].dtype)
    return out
```

```python
from contextlib import ExitStack

import concourse.bass as bass
from concourse import mybir

F32 = mybir.dt.float32
F32R = mybir.dt.float32r
BF16 = mybir.dt.bfloat16
U32 = mybir.dt.uint32
ALU = mybir.AluOpType
ACT = mybir.ActivationFunctionType
AX = mybir.AxisListType

P = 128
LN_EPS = 1e-5
NORM_EPS = 1e-12
GATE_FLOOR = 0.25
LOG_SMALLEST = -104.0


def at_least(engine, semaphore, count):
    if not isinstance(count, int) or count > 0:
        engine.wait_ge(semaphore, count)


def counted(engine, count):
    if not isinstance(count, int):
        engine.compute_val(count)
    return count


def adaln_block_kernel(nc, x, wq, bq, wk, bk, wv, bv, wo, bo, rel_ext, gate_v, gate_g, gate_b,
                       w1_v, w1_g, b1, w2_v, w2_g, b2, c, wmod, out):
    B, S, D = x.shape
    H = rel_ext.shape[0]
    DK = D // H
    E, HID, _ = w1_v.shape
    QT = S // P
    TILES = B * QT
    HT = 4
    QUADS = H // HT
    REP = P // (HT * DK)
    HC = HID // P
    GROUP = 512
    GT = GROUP // P
    GB = GROUP // S
    GROUPS = B * S // GROUP
    BW = S + P
    SCORE_SCALE = float(DK) ** -0.5
    assert D == P and S == 2 * P and HT * DK * REP == P and B == E and E == 8

    R_B1, R_W1G, R_W2G, R_B2 = 0, E * HC, 2 * E * HC, 2 * E * HC + E
    R_BQ = R_B2 + E
    R_BK, R_BV, R_BO, R_C = R_BQ + 1, R_BQ + 2, R_BQ + 3, R_BQ + 4
    ROWS = R_C + B

    with ExitStack() as ctx:
        def sb(name, shape, dt=F32):
            return ctx.enter_context(nc.sbuf_tensor(name, shape, dt))

        def sem(name):
            return ctx.enter_context(nc.semaphore(name))

        bank = [ctx.enter_context(nc.psum_tensor(f"bank{i}", [P, 512], F32)) for i in range(8)]
        score_bank, turned_bank = bank[0:2], bank[2:4]
        pv_bank, ot_bank, front_bank, tail_bank = bank[4:8]

        ident = sb("ident", [P, P])
        sel = sb("sel", [P, 4, QUADS, HT, REP, DK], F32R)
        w_raw = sb("w_raw", [P, 4, D])
        w_t = sb("w_t", [P, 4, D])
        rows = sb("rows", [P, D])
        cols = sb("cols", [P, ROWS])
        bq_scaled = sb("bq_scaled", [P, 1])
        silu_c = sb("silu_c", [P, 3, B])
        wmod_sb = sb("wmod_sb", [P, 6 * D])
        mod = sb("mod", [P, 6, B])
        gate_tmp = sb("gate_tmp", [P, 2, 2, B])
        ga_col = sb("ga_col", [P, 2, B])
        gb_col = sb("gb_col", [P, B])
        ga_row = sb("ga_row", [P, 2, B, D])
        band = sb("band", [P, H, BW])

        x_sb = sb("x_sb", [P, TILES, D])
        stats = sb("stats", [P, TILES, 6])
        mean_var = sb("mean_var", [P, TILES, 2])
        rstd = sb("rstd", [P, TILES])
        minus_half = sb("minus_half", [P, TILES])
        half = sb("half", [P, 8])

        normed = sb("normed", [P, QT, D])
        h_t = sb("h_t", [P, S])
        qk = sb("qk", [P, 2, S])
        qk_hi = sb("qk_hi", [P, 2, S], F32R)
        qk_lo = sb("qk_lo", [P, 2, S], F32R)
        stack = sb("stack", [P, QUADS, 2, S], F32R)
        v_wide = sb("v_wide", [P, QT, H, 32])
        ZR = 4
        z = sb("z", [P, ZR, QT, S])
        z_max = sb("z_max", [P, ZR, QT])
        w = sb("w", [P, ZR, QT, S])
        PR = 8
        probs = sb("probs", [P, PR, QT, S])
        ga_wide = probs[:, 0:PR // 2, :, :].rearrange("p (i u) t s -> p i (u t s)", i=2).rearrange(
            "p i (b c) -> p i b c", b=B)
        o_sb = sb("o_sb", [P, S])
        recip = sb("recip", [P, QT, HT])
        attn = sb("attn", [P, QT, D])
        attn_t = sb("attn_t", [P, S])
        gated = sb("gated", [P, QT, D])

        w1_raw = sb("w1_raw", [P, HC, D])
        w2_raw = sb("w2_raw", [P, HID])
        squares = sb("squares", [P, HID])
        norm_sq = sb("norm_sq", [P, 8])
        norm = sb("norm", [P, 8])
        norm_scale = sb("norm_scale", [P, 3, 8])
        w1_scaled = sb("w1_scaled", [P, HC, D])
        w2_scaled = sb("w2_scaled", [P, HID])
        w1_hi = sb("w1_hi", [P, E, HID], F32R)
        w1_lo = sb("w1_lo", [P, E, HID], F32R)
        w2_hi = sb("w2_hi", [P, E, HC, D], F32R)
        w2_lo = sb("w2_lo", [P, E, HC, D], F32R)

        gate_rows = sb("gate_rows", [E, D])
        gate_g_col = sb("gate_g_col", [E, 1])
        gate_b_row = sb("gate_b_row", [P, E])
        gate_sq = sb("gate_sq", [E, D])
        gate_norm = sb("gate_norm", [E, 4])
        gate_scaled = sb("gate_scaled", [E, D])
        gate_t = sb("gate_t", [P, E])
        stats2 = sb("stats2", [P, GT, 6])
        mean_var2 = sb("mean_var2", [P, GT, 2])
        rstd2 = sb("rstd2", [P, GT])
        choose = sb("choose", [E, E, P], BF16)
        expert_no = sb("expert_no", [P, GT, E])
        logits = sb("logits", [P, 3, GT, E])
        top = sb("top", [P, GT])
        top8 = sb("top8", [P, GT, 8])
        top_at = sb("top_at", [P, GT, 8], U32)
        top_no = sb("top_no", [P, GT, 2])
        chosen = sb("chosen", [P, 3, GT, E])
        mask_t = sb("mask_t", [E, GROUPS, GROUP], BF16)
        h_lo = sb("h_lo", [P, 2, GROUP], F32R)
        x_hi = stack[:, :, :, :].rearrange("p g i s -> p g (i s)")
        x_lo = sel[:, :, :, :, :, :].rearrange("p k g j r d -> p k (g j r d)")
        h_hi = [part[:, :, :].rearrange("p i s -> p (i s)") for part in (qk_hi, qk_lo)]
        normed2 = probs[:, 0, :, :].rearrange("p k (u d) -> p (k u) d", d=D)
        h2_t = probs[:, 1, :, :].rearrange("p k s -> p (k s)")
        spare = band[:, :, :].rearrange("p h u -> p (h u)").rearrange("p (i n) -> p i n", n=GROUP)
        hidden, mask_wide, masked = spare[:, 0:2, :], spare[:, 2:4, :], spare[:, 4:6, :]
        summed, gated2 = spare[:, 6, :], spare[:, 7, :]

        s_x = [sem(f"x_loaded{i}") for i in range(2)]
        s_w = sem("weights_loaded")
        s_rows = sem("rows_loaded")
        s_wmod = sem("wmod_loaded")
        s_band = [sem(f"band_loaded{i}") for i in range(QUADS)]
        s_exp_w = sem("expert_weights_loaded")
        s_ident0 = sem("ident_zeroed")
        s_ident = sem("ident_ready")
        s_consts = sem("pool_constants_ready")
        s_selz = sem("sel_zeroed")
        s_sel = sem("sel_ready")
        s_vz = sem("v_wide_zeroed")
        s_vinit = sem("v_wide_ready")
        s_rowsT = sem("rows_turned")
        s_cols = sem("cols_ready")
        s_wT_ps = sem("weights_turned")
        s_wT = sem("w_t_ready")
        s_cexp = sem("c_exp_done")
        s_sc = sem("silu_c_step")
        s_mod_ps = sem("mod_in_psum")
        s_mod = sem("mod_step")
        s_gaw = sem("ga_wide_ready")
        s_gar_ps = sem("ga_row_in_psum")
        s_gar = sem("ga_row_ready")
        s_stats = sem("stats_done")
        s_mv = sem("mean_var_done")
        s_eps = sem("eps_added")
        s_rstd = sem("rstd_done")

        s_norm = sem("normed_ready")
        s_hT_ps = sem("h_t_in_psum")
        s_hT = sem("h_t_ready")
        s_qk_ps = sem("qk_in_psum")
        s_qk = sem("qk_ready")
        s_hi = sem("qk_hi_ready")
        s_lo = sem("qk_lo_ready")
        s_rep_ps = sem("stack_in_psum")
        s_rep = sem("stack_ready")
        s_v_ps = sem("v_in_psum")
        s_v = sem("v_ready")
        s_xg = sem("x_plus_bias")
        s_score = sem("score_done")
        s_z = sem("z_ready")
        s_w_sub = sem("w_ready")
        s_t = sem("w_turned")
        s_p = sem("probs_ready")
        s_pv = sem("pv_done")
        s_o = sem("o_evacuated")
        s_oT = sem("o_turned")
        s_rc = sem("recip_done")
        s_at = sem("attn_ready")
        s_aT_ps = sem("attn_turned")
        s_aT = sem("attn_t_ready")
        s_y = sem("y_done")
        s_yg = sem("gated_done")
        s_x2 = sem("x2_ready")

        s_sq = sem("squares_done")
        s_nrm = sem("norm_done")
        s_ns = sem("norm_scale_step")
        s_ws = sem("w_scaled")
        s_w1T = sem("w1_turned")
        s_w2T = sem("w2_turned")
        s_w1h = sem("w1_hi_done")
        s_w2h = sem("w2_hi_done")
        s_w1l = sem("w1_lo_done")
        s_w2l = sem("w2_lo_done")
        s_out = sem("out_stored")

        s_gate_in = sem("gate_inputs_loaded")
        s_gsq = sem("gate_prep_step")
        s_gnorm = sem("gate_norm_done")
        s_gate_ps = sem("gate_t_in_psum")
        s_gate = sem("gate_t_ready")
        s_no = sem("expert_numbers_ready")
        s_choose = sem("choose_ready")
        s_stats2 = sem("stats2_done")
        s_eps2 = sem("eps2_step")
        s_rstd2 = sem("rstd2_done")
        s_norm2 = sem("normed2_ready")
        s_h2_ps = sem("h2_in_psum")
        s_h2 = sem("h2_ready")
        s_xhi = sem("x_hi_ready")
        s_xlo = sem("x_lo_ready")
        s_logit_ps = sem("logits_in_psum")
        s_logit = sem("logits_step")
        s_top = sem("top_step")
        s_chosen = sem("chosen_step")
        s_mask_ps = sem("mask_t_in_psum")
        s_mask = sem("mask_t_ready")
        s_wide_ps = sem("mask_wide_in_psum")
        s_wide = sem("mask_wide_ready")
        s_l1 = sem("hidden_in_psum")
        s_silu = sem("hidden_ready")
        s_hhi = sem("h_hi_ready")
        s_hlo = sem("h_lo_ready")
        s_l2 = sem("l2_done")
        s_masked = sem("masked_ready")
        s_sum = sem("summed_step")
        s_gated2 = sem("gated2_ready")
        s_back = sem("gated2_turned")
        s_final = sem("final_ready")

        block = ctx.enter_context(nc.Block())
        x_dram = x.rearrange("b (t p) d -> p (b t) d", p=P)
        w1_dram = w1_v.rearrange("e (k p) d -> p (e k) d", p=P)
        w2_dram = w2_v.rearrange("e d h -> d e h")
        out_dram = out.rearrange("b (t p) d -> p (b t) d", p=P)

        def row(v):
            return v.rearrange("(a d) -> a d", a=1)

        def band_dram(g):
            width = rel_ext.shape[1]
            return bass.AP(rel_ext.tensor, HT * g * width, [[1, P], [width, HT], [1, BW]])

        def batches(engine, step):
            step(0, True, False, True)
            with engine.Fori(1, B - 1) as b:
                step(b, True, True, True)
            step(B - 1, True, True, False)
            step(B, False, True, False)

        N1 = E * HC

        def groups(engine, step):
            step(0, True, False, True)
            with engine.Fori(1, GROUPS - 1) as g:
                step(g, True, True, True)
            step(GROUPS - 1, True, True, False)
            step(GROUPS, False, True, False)

        @block.sync
        def _(sp):
            sp.dma_start(x_sb[:, 0:QT, :], x_dram[:, 0:QT, :]).then_inc(s_x[0], 16)
            for i, a in enumerate((wq, wk, wv, wo)):
                sp.dma_start(w_raw[:, i, :], a).then_inc(s_w, 16)
            sp.dma_start(x_sb[:, QT:TILES, :], x_dram[:, QT:TILES, :]).then_inc(s_x[1], 16)
            for g in range(QUADS):
                sp.dma_start(band[:, HT * g:HT * (g + 1), :], band_dram(g)).then_inc(s_band[g], 16)

            def load_expert(e):
                sp.dma_start(w1_raw[:, :, :], w1_dram[:, bass.ds(e * HC, HC), :]).then_inc(s_exp_w, 16)
                sp.dma_start(w2_raw[:, :], w2_dram[:, bass.ds(e, 1), :]).then_inc(s_exp_w, 16)

            load_expert(0)
            with sp.Fori(1, E) as e:
                sp.wait_ge(s_ws, 2 * e)
                load_expert(e)
            sp.wait_ge(s_final, 1)
            sp.dma_start(out_dram[:, 0:GT, :], x_sb[:, 0:GT, :]).then_inc(s_out, 16)
            with sp.Fori(1, GROUPS) as g:
                sp.wait_ge(s_final, g + 1)
                sp.dma_start(out_dram[:, bass.ds(g * GT, GT), :],
                             x_sb[:, bass.ds(g * GT, GT), :]).then_inc(s_out, 16)
            sp.wait_ge(s_out, 16 * GROUPS)

        @block.gpsimd
        def _(pool):
            pool.memset(ident[:, :], 0.0).then_inc(s_ident0, 1)
            pool.memset(minus_half[:, :], -0.5).then_inc(s_consts, 1)
            pool.memset(half[:, :], 0.5).then_inc(s_consts, 1)
            pool.wait_ge(s_ident0, 1)
            pool.affine_select(out=ident[:, :], in_=ident[:, :], compare_op=ALU.not_equal, fill=1.0, base=0,
                               pattern=[[-1, P]], channel_multiplier=1).then_inc(s_ident, 1)
            pool.wait_ge(s_consts, 2)
            for i, (a, e) in enumerate(((0, QT), (QT, TILES))):
                if i == 1:
                    pool.memset(sel[:, :, :, :, :, :].bitcast(F32), 0.0).then_inc(s_selz, 1)
                    pool.wait_ge(s_selz, 1)
                    pool.wait_ge(s_ident, 1)
                    ones = ident[:, :].rearrange("p (g j d) -> p g j d", g=QUADS, j=HT)
                    for k, reps in enumerate(((0, 1), (2, 3), (0, 2), (1, 3))):
                        for r in reps:
                            pool.tensor_copy(sel[:, k, :, :, r, :], ones).then_inc(s_sel, 1)
                    pool.memset(v_wide[:, :, :, :], 0.0).then_inc(s_vz, 1)
                    pool.wait_ge(s_vz, 1)
                    pool.memset(v_wide[:, :, :, DK:DK + 1], 1.0).then_inc(s_vinit, 1)
                    pool.iota(expert_no[:, :, :], pattern=[[0, GT], [1, E]], base=0, channel_multiplier=0,
                              allow_small_or_imprecise_dtypes=True).then_inc(s_no, 1)
                    pool.tensor_copy(choose[:, :, :], ident[0:E, 0:E].unsqueeze(2).to_broadcast([E, E, P])).then_inc(s_choose, 1)
                pool.wait_ge(s_eps, i + 1)
                pool.tensor_tensor(rstd[:, a:e], mean_var[:, a:e, 1], minus_half[:, a:e],
                                   ALU.pow).then_inc(s_rstd, 1)
            pool.wait_ge(s_gsq, 1)
            pool.tensor_tensor(gate_norm[:, 1:2], gate_norm[:, 0:1], half[0:E, 0:1], ALU.pow).then_inc(s_gnorm, 1)

            def step(b, own, prev, nxt):
                if not own:
                    return
                for h in range(H):
                    n = b * H + h
                    ready, turned = counted(pool, n + 1), counted(pool, n - ZR + 1)
                    pool.wait_ge(s_consts, 2)
                    pool.wait_ge(s_z, ready)
                    at_least(pool, s_t, turned)
                    for qt in range(QT):
                        sub = pool.tensor_scalar(w[:, h % ZR, qt, :], z[:, h % ZR, qt, :], -1.0,
                                                 z_max[:, h % ZR, qt:qt + 1], ALU.mult, ALU.add)
                    sub.then_inc(s_w_sub, 1)
                    if h == 3:
                        pool.wait_ge(s_sq, (b + 1) * (HC + 1))
                        at_least(pool, s_ns, 3 * b)
                        pool.tensor_tensor(norm[:, 0:HC + 1], norm_sq[:, 0:HC + 1], half[:, 0:HC + 1],
                                           ALU.pow).then_inc(s_nrm, 1)
                    if h == 6:
                        pool.wait_ge(s_gar, 4)
                        pool.wait_ge(s_norm, b + 1)
                        for qt in range(QT):
                            tile = x_sb[:, bass.ds(b * QT + qt, 1), :]
                            add = pool.tensor_tensor(tile, tile, ga_row[:, 1, bass.ds(b, 1), :], ALU.add)
                        add.then_inc(s_xg, 1)

            batches(pool, step)

            def front(g):
                pool.wait_ge(s_eps2, 2 * g + 2)
                pool.tensor_tensor(rstd2[:, :], mean_var2[:, :, 1], minus_half[:, 0:GT], ALU.pow).then_inc(s_rstd2, 1)

            def expert_step(g, own, prev, nxt):
                if prev:
                    e = E - 1
                    done = (E - 1) * (g - 1)
                    pool.wait_ge(s_masked, E * g)
                    pool.wait_ge(s_sum, done + e - 1)
                    pool.tensor_tensor(summed, summed, masked[:, e % 2, :], ALU.add).then_inc(s_sum, 1)
                if not own:
                    return
                for e in range(1, E - 1):
                    done = (E - 1) * g
                    pool.wait_ge(s_masked, E * g + e + 1)
                    at_least(pool, s_sum, done + e - 1)
                    pool.tensor_tensor(summed, summed, masked[:, e % 2, :], ALU.add).then_inc(s_sum, 1)
                    if nxt and e == 2:
                        front(g + 1)

            front(0)
            groups(pool, expert_step)

        @block.vector
        def _(dve):
            def norm_stats(a, e):
                for t in range(a, e):
                    dve.bn_stats(stats[:, t, :], x_sb[:, t, :]).then_inc(s_stats, 1)
                dve.wait_ge(s_stats, e)
                for t in range(a, e):
                    dve.bn_aggr(mean_var[:, t, :], stats[:, t, :]).then_inc(s_mv, 1)
                dve.wait_ge(s_mv, e)
                dve.tensor_scalar(mean_var[:, a:e, 1], mean_var[:, a:e, 1], LN_EPS, None,
                                  ALU.add).then_inc(s_eps, 1)

            def make_normed(b):
                at_least(dve, s_hT_ps, b)
                for qt in range(QT):
                    t = b * QT + qt
                    last = dve.tensor_scalar(normed[:, qt, :], x_sb[:, bass.ds(t, 1), :],
                                             mean_var[:, bass.ds(t, 1), 0], rstd[:, bass.ds(t, 1)],
                                             ALU.subtract, ALU.mult)
                last.then_inc(s_norm, 1)

            def make_h_t(b):
                dve.wait_ge(s_hT_ps, b + 1)
                at_least(dve, s_v_ps, b)
                dve.tensor_scalar(h_t[:, :], front_bank[:, 0:S], mod[:, 1, bass.ds(b, 1)],
                                  mod[:, 0, bass.ds(b, 1)], ALU.mult, ALU.add).then_inc(s_hT, 1)

            def split_hi(b):
                dve.wait_ge(s_qk, 2 * (b + 1))
                at_least(dve, s_rep_ps, QUADS * b)
                dve.tensor_copy(qk_hi[:, :, :], qk[:, :, :]).then_inc(s_hi, 1)

            def split_lo(b):
                dve.wait_ge(s_hi, b + 1)
                dve.tensor_tensor(qk_lo[:, :, :], qk[:, :, :], qk_hi[:, :, :].bitcast(F32),
                                  ALU.subtract).then_inc(s_lo, 1)

            dve.wait_ge(s_x[0], 16)
            norm_stats(0, QT)
            dve.wait_ge(s_rowsT, 1)
            dve.tensor_copy(cols[:, :], bank[1][:, 0:ROWS]).then_inc(s_cols, 1)
            dve.wait_ge(s_cols, 1)
            dve.tensor_scalar(bq_scaled[:, :], cols[:, R_BQ:R_BQ + 1], SCORE_SCALE, None, ALU.mult).then_inc(s_cols, 1)
            dve.wait_ge(s_cexp, 1)
            dve.tensor_scalar(silu_c[:, 1, :], silu_c[:, 0, :], 1.0, None, ALU.add).then_inc(s_sc, 1)
            dve.wait_ge(s_sc, 1)
            dve.reciprocal(silu_c[:, 2, :], silu_c[:, 1, :]).then_inc(s_sc, 1)
            dve.wait_ge(s_sc, 2)
            dve.tensor_tensor(silu_c[:, 0, :], silu_c[:, 2, :], cols[:, R_C:R_C + B], ALU.mult).then_inc(s_sc, 1)
            dve.wait_ge(s_rstd, 1)
            make_normed(0)
            dve.wait_ge(s_mod_ps, 1)
            dve.tensor_copy(mod[:, :, :], bank[2][:, 0:6 * B].rearrange("p (j b) -> p j b", j=6)).then_inc(s_mod, 1)
            dve.wait_ge(s_mod, 1)
            for j in (1, 4):
                dve.tensor_scalar(mod[:, j, :], mod[:, j, :], 1.0, None, ALU.add).then_inc(s_mod, 1)
            dve.wait_ge(s_mod, 3)
            make_h_t(0)
            for i, j in enumerate((2, 5)):
                g = mod[:, j, :]
                dve.tensor_scalar(gate_tmp[:, i, 0, :], g, 0.0, 2.0, ALU.is_ge, ALU.mult).then_inc(s_mod, 1)
                dve.scalar_tensor_tensor(out=gate_tmp[:, i, 1, :], in0=g, scalar=-1.0, in1=g, op0=ALU.mult,
                                         op1=ALU.max).then_inc(s_mod, 1)
            dve.wait_ge(s_mod, 7)
            for i in range(2):
                dve.tensor_scalar(gate_tmp[:, i, 1, :], gate_tmp[:, i, 1, :], GATE_FLOOR, None,
                                  ALU.max).then_inc(s_mod, 1)
            dve.wait_ge(s_mod, 9)
            for i, o in enumerate((ga_col[:, 0, :], gb_col[:, :])):
                dve.scalar_tensor_tensor(out=o, in0=gate_tmp[:, i, 0, :], scalar=-1.0, in1=gate_tmp[:, i, 1, :],
                                         op0=ALU.add, op1=ALU.mult).then_inc(s_mod, 1)
            split_hi(0)
            dve.wait_ge(s_mod, 11)
            dve.tensor_scalar(ga_col[:, 1, :], ga_col[:, 0, :], cols[:, R_BO:R_BO + 1], None,
                              ALU.mult).then_inc(s_mod, 1)
            split_lo(0)
            dve.wait_ge(s_mod, 12)
            dve.tensor_copy(ga_wide[:, :, :, :], ga_col[:, :, :].unsqueeze(3).to_broadcast([P, 2, B, P])).then_inc(s_gaw, 1)
            dve.wait_ge(s_x[1], 16)
            norm_stats(QT, TILES)
            dve.wait_ge(s_gate_in, 48)
            dve.tensor_tensor_reduce(gate_sq[:, :], gate_rows[:, :], gate_rows[:, :], 1.0, 0.0, ALU.mult, ALU.add,
                                     gate_norm[:, 0:1]).then_inc(s_gsq, 1)
            dve.wait_ge(s_gnorm, 1)
            dve.tensor_scalar(gate_norm[:, 2:3], gate_norm[:, 1:2], NORM_EPS, None, ALU.max).then_inc(s_gsq, 1)
            dve.wait_ge(s_gsq, 2)
            dve.reciprocal(gate_norm[:, 3:4], gate_norm[:, 2:3]).then_inc(s_gsq, 1)
            dve.wait_ge(s_gsq, 3)
            dve.tensor_scalar(gate_scaled[:, :], gate_rows[:, :], gate_norm[:, 3:4], gate_g_col[:, 0:1], ALU.mult,
                              ALU.mult).then_inc(s_gsq, 1)

            def step(b, own, prev, nxt):
                for h in range(H):
                    n = b * H + h
                    if own:
                        scored, subtracted = counted(dve, n + 1), counted(dve, n - ZR + 1)
                        dve.wait_ge(s_band[h // HT], 16)
                        dve.wait_ge(s_score, scored)
                        at_least(dve, s_w_sub, subtracted)
                        for qt in range(QT):
                            last_key = qt * P
                            last = dve.tensor_tensor_reduce(
                                z[:, h % ZR, qt, :], score_bank[h % 2][:, qt * S:(qt + 1) * S],
                                band[:, h, last_key:last_key + S][:, ::-1], 1.0, -3.0e38, ALU.add, ALU.max,
                                z_max[:, h % ZR, qt:qt + 1])
                        last.then_inc(s_z, 1)
                    if (prev and h in (1, 5)) or (own and h in (9, 13)):
                        quad = b * QUADS + (h - 1) // 4 - 2
                        g = ((h - 1) // 4 + 2) % QUADS
                        turned = ot_bank[:, 0:S].rearrange("p (t j c) -> p t j c", t=QT, j=HT)
                        dve.wait_ge(s_oT, quad + 1)
                        dve.reciprocal(recip[:, :, :], turned[:, :, :, DK]).then_inc(s_rc, 1)
                        dve.wait_ge(s_rc, quad + 1)
                        if h == 9:
                            at_least(dve, s_aT_ps, b)
                        dst = attn[:, :, :].rearrange("p t (g j d) -> p t g j d", g=QUADS, j=HT)
                        dve.tensor_tensor(dst[:, :, g, :, :], turned[:, :, :, 0:DK],
                                          recip[:, :, :].unsqueeze(3).to_broadcast([P, QT, HT, DK]),
                                          ALU.mult).then_inc(s_at, 1)
                    if nxt and h == 4:
                        if isinstance(b, int) and b == 0:
                            dve.wait_ge(s_rstd, 2)
                        make_normed(b + 1)
                    if own and h == 5:
                        dve.wait_ge(s_v_ps, b + 1)
                        at_least(dve, s_pv, QUADS * b)
                        if isinstance(b, int) and b == 0:
                            dve.wait_ge(s_vinit, 1)
                        dve.tensor_copy(v_wide[:, :, :, 0:DK], front_bank[:, 0:QT * D].rearrange(
                            "p (t h d) -> p t h d", t=QT, h=H)).then_inc(s_v, 1)
                    if own and h == 4:
                        dve.wait_ge(s_nrm, b + 1)
                        dve.tensor_scalar(norm_scale[:, 0, 0:HC + 1], norm[:, 0:HC + 1], NORM_EPS, None,
                                          ALU.max).then_inc(s_ns, 1)
                        dve.wait_ge(s_ns, 3 * b + 1)
                        dve.reciprocal(norm_scale[:, 1, 0:HC + 1], norm_scale[:, 0, 0:HC + 1]).then_inc(s_ns, 1)
                    if own and h == 6:
                        dve.wait_ge(s_ns, 3 * b + 2)
                        at_least(dve, s_ws, 2 * b)
                        dve.tensor_tensor(norm_scale[:, 2, 0:HC], norm_scale[:, 1, 0:HC],
                                          cols[:, bass.ds(R_W1G + b * HC, HC)], ALU.mult)
                        dve.tensor_tensor(norm_scale[:, 2, HC:HC + 1], norm_scale[:, 1, HC:HC + 1],
                                          cols[:, bass.ds(R_W2G + b, 1)], ALU.mult).then_inc(s_ns, 1)
                        dve.wait_ge(s_ns, 3 * b + 3)
                        at_least(dve, s_w1T, b)
                        dve.tensor_tensor(w1_scaled[:, :, :], w1_raw[:, :, :],
                                          norm_scale[:, 2, 0:HC].unsqueeze(2).to_broadcast([P, HC, D]),
                                          ALU.mult).then_inc(s_ws, 1)
                    if own and h == 7:
                        at_least(dve, s_w2T, b)
                        dve.tensor_scalar(w2_scaled[:, :], w2_raw[:, :],
                                          norm_scale[:, 2, HC:HC + 1], None, ALU.mult).then_inc(s_ws, 1)
                    if nxt and h == 7:
                        make_h_t(b + 1)
                    if prev and h == 8:
                        dve.wait_ge(s_y, b)
                        dve.tensor_tensor(gated[:, :, :], tail_bank[:, S:2 * S].rearrange("p (t d) -> p t d", t=QT),
                                          ga_row[:, 0, bass.ds(b - 1, 1), :].to_broadcast([P, QT, D]),
                                          ALU.mult).then_inc(s_yg, 1)
                        dve.wait_ge(s_yg, b)
                        dve.wait_ge(s_xg, b)
                        dve.tensor_tensor(x_sb[:, bass.ds((b - 1) * QT, QT), :], x_sb[:, bass.ds((b - 1) * QT, QT), :],
                                          gated[:, :, :], ALU.add).then_inc(s_x2, 1)
                    if nxt and h == 9:
                        split_hi(b + 1)
                    if nxt and h == 10:
                        split_lo(b + 1)
                    if own and h == 11:
                        dve.wait_ge(s_w1h, b + 1)
                        dve.tensor_tensor(w1_lo[:, bass.ds(b, 1), :], tail_bank[:, :].unsqueeze(1),
                                          w1_hi[:, bass.ds(b, 1), :].bitcast(F32), ALU.subtract).then_inc(s_w1l, 1)
                    if own and h == 15:
                        dve.wait_ge(s_w2h, b + 1)
                        dve.tensor_tensor(w2_lo[:, bass.ds(b, 1), :, :],
                                          tail_bank[:, :].rearrange("p (a k d) -> p a k d", a=1, k=HC),
                                          w2_hi[:, bass.ds(b, 1), :, :].bitcast(F32), ALU.subtract).then_inc(s_w2l, 1)

            batches(dve, step)

            def front_stats(g):
                for t in range(GT):
                    last = dve.bn_stats(stats2[:, t, :], x_sb[:, bass.ds(g * GT + t, 1), :])
                last.then_inc(s_stats2, 1)
                seen = counted(dve, g + 1)
                dve.wait_ge(s_no, 1)
                dve.wait_ge(s_stats2, seen)
                for t in range(GT):
                    last = dve.bn_aggr(mean_var2[:, t, :], stats2[:, t, :])
                last.then_inc(s_eps2, 1)
                dve.wait_ge(s_eps2, 2 * g + 1)
                dve.tensor_scalar(mean_var2[:, :, 1], mean_var2[:, :, 1], LN_EPS, None, ALU.add).then_inc(s_eps2, 1)

            def front_normed(g):
                dve.wait_ge(s_rstd2, g + 1)
                at_least(dve, s_h2_ps, g)
                for t in range(GT):
                    last = dve.tensor_scalar(normed2[:, t, :], x_sb[:, bass.ds(g * GT + t, 1), :],
                                             mean_var2[:, t, 0:1], rstd2[:, t:t + 1], ALU.subtract, ALU.mult)
                last.then_inc(s_norm2, 1)

            def front_h2(g):
                dve.wait_ge(s_h2_ps, g + 1)
                at_least(dve, s_logit_ps, g)
                for i in range(GB):
                    b = bass.ds(g * GB + i, 1)
                    last = dve.tensor_scalar(h2_t[:, i * S:(i + 1) * S], bank[5][:, i * S:(i + 1) * S], mod[:, 4, b],
                                             mod[:, 3, b], ALU.mult, ALU.add)
                last.then_inc(s_h2, 1)

            def front_hi(g):
                dve.wait_ge(s_h2, g + 1)
                dve.tensor_copy(x_hi[:, bass.ds(g, 1), :], h2_t[:, :].unsqueeze(1)).then_inc(s_xhi, 1)

            def front_lo(g):
                dve.wait_ge(s_xhi, g + 1)
                dve.tensor_tensor(x_lo[:, bass.ds(g, 1), :], h2_t[:, :].unsqueeze(1),
                                  x_hi[:, bass.ds(g, 1), :].bitcast(F32), ALU.subtract).then_inc(s_xlo, 1)

            def front_gates(g, part):
                wide = [P, GT, E]
                if part == 0:
                    dve.wait_ge(s_logit_ps, g + 1)
                    dve.tensor_tensor(logits[:, 0, :, :], bank[7][:, 0:GT * E].rearrange("p (t e) -> p t e", t=GT),
                                      gate_b_row[:, :].unsqueeze(1).to_broadcast(wide), ALU.add).then_inc(s_logit, 1)
                    dve.wait_ge(s_logit, 4 * g + 1)
                    dve.tensor_reduce(top[:, :], logits[:, 0, :, :], AX.X, ALU.max).then_inc(s_logit, 1)
                    dve.wait_ge(s_logit, 4 * g + 2)
                    dve.tensor_tensor(logits[:, 1, :, :], logits[:, 0, :, :],
                                      top[:, :].unsqueeze(2).to_broadcast(wide), ALU.subtract).then_inc(s_logit, 1)
                    dve.wait_ge(s_logit, 4 * g + 3)
                    dve.tensor_scalar(logits[:, 2, :, :], logits[:, 1, :, :], LOG_SMALLEST, None,
                                      ALU.max).then_inc(s_logit, 1)
                if part == 1:
                    seen = counted(dve, 4 * g + 4)
                    dve.wait_ge(s_no, 1)
                    dve.wait_ge(s_logit, seen)
                    for t in range(GT):
                        last = dve.max(top8[:, t, :], logits[:, 2, t, :])
                    last.then_inc(s_top, 1)
                    seen = counted(dve, 3 * g + 1)
                    dve.wait_ge(s_no, 1)
                    dve.wait_ge(s_top, seen)
                    for t in range(GT):
                        last = dve.max_index(top_at[:, t, :], top8[:, t, :], logits[:, 2, t, :])
                    last.then_inc(s_top, 1)
                    dve.wait_ge(s_top, 3 * g + 2)
                    dve.tensor_copy(top_no[:, :, :], top_at[:, :, 0:2]).then_inc(s_top, 1)
                if part == 2:
                    dve.wait_ge(s_top, 3 * g + 3)
                    at_least(dve, s_mask_ps, g)
                    for k in range(2):
                        last = dve.tensor_tensor(chosen[:, k, :, :], expert_no[:, :, :],
                                                 top_no[:, :, k].unsqueeze(2).to_broadcast(wide), ALU.is_equal)
                    last.then_inc(s_chosen, 1)
                    dve.wait_ge(s_chosen, 2 * g + 1)
                    dve.tensor_tensor(chosen[:, 2, :, :], chosen[:, 0, :, :], chosen[:, 1, :, :],
                                      ALU.add).then_inc(s_chosen, 1)

            def expert_step(g, own, prev, nxt):
                for t in range(N1):
                    if own:
                        dve.wait_ge(s_hhi, N1 * g + t + 1)
                        dve.tensor_tensor(h_lo[:, t % 2, :], hidden[:, t % 2, :], h_hi[t % 2].bitcast(F32),
                                          ALU.subtract).then_inc(s_hlo, 1)
                    if (own and t % HC == 1 and t > 1) or (prev and t == 1):
                        e = ((t - 1) // HC - 1) % E
                        no = E * g + (t - 1) // HC - 1
                        dve.wait_ge(s_l2, HC * (no + 1))
                        dve.wait_ge(s_wide, no + 1)
                        if e == 0:
                            at_least(dve, s_gated2, g)
                        elif t == 1:
                            dve.wait_ge(s_sum, (E - 1) * (g - 1) + e - 2)
                        else:
                            at_least(dve, s_sum, (E - 1) * g + max(e - 2, 0))
                        dve.scalar_tensor_tensor(out=summed if e == 0 else masked[:, e % 2, :],
                                                 in0=bank[2 + e % 2][:, :], scalar=cols[:, R_B2 + e:R_B2 + e + 1],
                                                 in1=mask_wide[:, e % 2, :], op0=ALU.add,
                                                 op1=ALU.mult).then_inc(s_masked, 1)
                    if prev and t == 7:
                        dve.wait_ge(s_back, g)
                        at = bass.ds((g - 1) * GT, GT)
                        dve.tensor_tensor(x_sb[:, at, :], x_sb[:, at, :],
                                          bank[6][:, :].rearrange("p (t d) -> p t d", t=GT), ALU.add).then_inc(s_final, 1)
                    if nxt and t == 9:
                        front_stats(g + 1)
                    if nxt and t == 14:
                        front_normed(g + 1)
                    if nxt and t == 16:
                        front_h2(g + 1)
                    if nxt and t == 18:
                        front_hi(g + 1)
                    if nxt and t == 20:
                        front_lo(g + 1)
                    if nxt and t in (22, 24, 26):
                        front_gates(g + 1, (t - 22) // 2)

            dve.wait_ge(s_gate_ps, 1)
            dve.tensor_copy(gate_t[:, :], bank[7][:, 0:E]).then_inc(s_gate, 1)
            dve.wait_ge(s_x2, B)
            front_stats(0)
            front_normed(0)
            front_h2(0)
            front_hi(0)
            front_lo(0)
            for part in range(3):
                front_gates(0, part)
            groups(dve, expert_step)

        @block.scalar
        def _(act):
            rows_in = ((R_B1, E * HC, b1.rearrange("e (k d) -> (e k) d", d=D)),
                       (R_W1G, E * HC, w1_g.rearrange("e (k d) -> (e k) d", d=D)),
                       (R_W2G, E, w2_g), (R_B2, E, b2), (R_BQ, 1, row(bq)), (R_BK, 1, row(bk)),
                       (R_BV, 1, row(bv)), (R_BO, 1, row(bo)), (R_C, B, c))
            for at, n, src in rows_in:
                act.dma_start(rows[at:at + n, :], src).then_inc(s_rows, 16)
            act.dma_start(wmod_sb[:, :], wmod).then_inc(s_wmod, 16)
            act.dma_start(gate_rows[:, :], gate_v).then_inc(s_gate_in, 16)
            act.dma_start(gate_g_col[:, :], gate_g.rearrange("(e a) -> e a", a=1)).then_inc(s_gate_in, 16)
            act.dma_start(gate_b_row[:, :], bass.AP(gate_b.tensor, 0, [[0, P], [1, E]])).then_inc(s_gate_in, 16)
            act.wait_ge(s_cols, 1)
            act.activation(silu_c[:, 0, :], cols[:, R_C:R_C + B], ACT.Exp, scale=-1.0).then_inc(s_cexp, 1)
            act.wait_ge(s_wT_ps, 1)
            act.activation(w_t[:, :, :], bank[0][:, :].rearrange("p (i d) -> p i d", i=4), ACT.Copy).then_inc(s_wT, 1)

            def evacuate_qk(b):
                act.wait_ge(s_qk_ps, b + 1)
                at_least(act, s_lo, b)
                act.activation(qk[:, 0, :], front_bank[:, 0:S], ACT.Identity, bias=bq_scaled[:, 0:1],
                               scale=SCORE_SCALE).then_inc(s_qk, 1)
                act.activation(qk[:, 1, :], front_bank[:, S:2 * S], ACT.Identity,
                               bias=cols[:, R_BK:R_BK + 1]).then_inc(s_qk, 1)

            def evacuate_stack(b, g):
                act.wait_ge(s_rep_ps, QUADS * b + g + 1)
                at_least(act, s_score, H * (b - 1) + HT * (g + 1))
                act.activation(stack[:, g, :, :], front_bank[:, :].rearrange("p (i s) -> p i s", i=2),
                               ACT.Copy).then_inc(s_rep, 1)

            act.wait_ge(s_cols, 2)
            evacuate_qk(0)
            for g in range(QUADS - 1):
                evacuate_stack(0, g)
            for i in range(2):
                for half_b in range(2):
                    act.wait_ge(s_gar_ps, 2 * i + half_b + 1)
                    act.activation(ga_row[:, i, half_b * B // 2:(half_b + 1) * B // 2, :],
                                   bank[2 + 2 * i + half_b][:, :].rearrange("p (b d) -> p b d", b=B // 2),
                                   ACT.Copy).then_inc(s_gar, 1)

            def step(b, own, prev, nxt):
                for h in range(H):
                    if (own and h >= 3) or (prev and h < 3):
                        n = b * H + h - 3
                        slot = (h - 3) % PR
                        act.wait_ge(s_t, n + 1)
                        if slot % HT == 0:
                            at_least(act, s_pv, b * QUADS + (h - 3) // HT - 1)
                        act.activation(probs[:, slot, :, :],
                                       turned_bank[(h - 3) % 2][:, :].rearrange("p (k q) -> p k q", k=QT),
                                       ACT.Exp, scale=-1.0).then_inc(s_p, 1)
                    if (prev and h == 3) or (own and h in (7, 11, 15)):
                        quad = b * QUADS + (h - 7) // 4
                        act.wait_ge(s_pv, quad + 1)
                        at_least(act, s_oT, quad)
                        act.activation(o_sb[:, :], pv_bank[:, 0:S], ACT.Copy).then_inc(s_o, 1)
                    if own and h == 0:
                        act.wait_ge(s_exp_w, 32 * (b + 1))
                        at_least(act, s_nrm, b)
                        for k in range(HC):
                            act.activation(squares[:, k * D:(k + 1) * D], w1_raw[:, k, :],
                                           ACT.Square, accum_out=norm_sq[:, k:k + 1]).then_inc(s_sq, 1)
                    if own and h == 2:
                        act.wait_ge(s_sq, (HC + 1) * b + HC)
                        act.activation(squares[:, :], w2_raw[:, :], ACT.Square,
                                       accum_out=norm_sq[:, HC:HC + 1]).then_inc(s_sq, 1)
                    if own and h == 1:
                        evacuate_stack(b, QUADS - 1)
                    if prev and h == 6:
                        act.wait_ge(s_aT_ps, b)
                        act.activation(attn_t[:, :], tail_bank[:, 0:S], ACT.Identity,
                                       bias=cols[:, R_BV:R_BV + 1]).then_inc(s_aT, 1)
                    if nxt and h == 8:
                        evacuate_qk(b + 1)
                    if own and h == 10:
                        act.wait_ge(s_w1T, b + 1)
                        act.activation(w1_hi[:, bass.ds(b, 1), :], tail_bank[:, :].unsqueeze(1),
                                       ACT.Copy).then_inc(s_w1h, 1)
                    if nxt and h in (11, 12, 13):
                        evacuate_stack(b + 1, h - 11)
                    if own and h == 14:
                        act.wait_ge(s_w2T, b + 1)
                        act.activation(w2_hi[:, bass.ds(b, 1), :, :],
                                       tail_bank[:, :].rearrange("p (a k d) -> p a k d", a=1, k=HC),
                                       ACT.Copy).then_inc(s_w2h, 1)

            batches(act, step)

            def front_mask(g):
                act.wait_ge(s_mask_ps, g + 1)
                act.activation(mask_t[:, bass.ds(g, 1), :], bank[7][0:E, :].unsqueeze(1), ACT.Copy).then_inc(s_mask, 1)

            def expert_step(g, own, prev, nxt):
                for t in range(N1):
                    if own:
                        e = t // HC
                        no = N1 * g + t
                        act.wait_ge(s_l1, no + 1)
                        at_least(act, s_hlo, no - 1)
                        act.activation(hidden[:, t % 2, :], bank[t % 2][:, :], ACT.Silu,
                                       bias=cols[:, R_B1 + t:R_B1 + t + 1]).then_inc(s_silu, 1)
                        act.wait_ge(s_silu, no + 1)
                        at_least(act, s_l2, no - 1)
                        act.activation(h_hi[t % 2], hidden[:, t % 2, :], ACT.Copy).then_inc(s_hhi, 1)
                        if t % HC == 0:
                            act.wait_ge(s_wide_ps, E * g + e + 1)
                            at_least(act, s_masked, E * g + e - 1)
                            act.activation(mask_wide[:, e % 2, :], bank[4][:, :], ACT.Copy).then_inc(s_wide, 1)
                    if prev and t == 3:
                        act.wait_ge(s_sum, (E - 1) * g)
                        at_least(act, s_back, g - 1)
                        for i in range(GB):
                            last = act.activation(gated2[:, i * S:(i + 1) * S], summed[:, i * S:(i + 1) * S],
                                                  ACT.Copy, scale=gb_col[:, bass.ds((g - 1) * GB + i, 1)])
                        last.then_inc(s_gated2, 1)
                    if nxt and t == 28:
                        front_mask(g + 1)

            front_mask(0)
            groups(act, expert_step)

        @block.tensor
        def _(pe):
            def turn(dst, src, n=P):
                return pe.transpose(dst, src, ident[0:n, 0:n])

            def turn_normed(b):
                pe.wait_ge(s_norm, b + 1)
                at_least(pe, s_v, b)
                for qt in range(QT):
                    last = turn(front_bank[:, qt * P:(qt + 1) * P], normed[:, qt, :])
                last.then_inc(s_hT_ps, 1)

            def project_qk(b):
                pe.wait_ge(s_hT, b + 1)
                for i in range(2):
                    last = pe.matmul(front_bank[:, i * S:(i + 1) * S], w_t[:, i, :], h_t[:, :], start=True, stop=True)
                last.then_inc(s_qk_ps, 1)

            def make_stack(b, g):
                pe.wait_ge(s_lo, b + 1)
                at_least(pe, s_rep, QUADS * b + g)
                for i in range(2):
                    for part, lo in ((qk_hi, 0), (qk_lo, 1)):
                        choose = sel[:, 2 * i + lo, g, :, :, :].rearrange("p j r d -> p (j r d)")
                        last = pe.matmul(front_bank[:, i * S:(i + 1) * S], choose, part[:, i, :],
                                         start=(lo == 0), stop=(lo == 1))
                last.then_inc(s_rep_ps, 1)

            pe.wait_ge(s_ident, 1)
            pe.wait_ge(s_rows, 16 * 9)
            turn(bank[1][:, 0:ROWS], rows[0:ROWS, :], ROWS).then_inc(s_rowsT, 1)
            pe.wait_ge(s_w, 64)
            for i in range(4):
                last = turn(bank[0][:, i * P:(i + 1) * P], w_raw[:, i, :])
            last.then_inc(s_wT_ps, 1)
            turn_normed(0)
            pe.wait_ge(s_wmod, 16)
            pe.wait_ge(s_sc, 3)
            for j in range(6):
                last = pe.matmul(bank[2][:, j * B:(j + 1) * B], wmod_sb[:, j * D:(j + 1) * D], silu_c[:, 0, :],
                                 start=True, stop=True)
            last.then_inc(s_mod_ps, 1)
            pe.wait_ge(s_wT, 1)
            project_qk(0)
            pe.wait_ge(s_sel, 8)
            for g in range(QUADS - 1):
                make_stack(0, g)
            pe.wait_ge(s_gaw, 1)
            for i in range(2):
                for b in range(B):
                    last = pe.matmul(bank[2 + 2 * i + b // 4][:, (b % 4) * P:(b % 4 + 1) * P], ga_wide[:, i, b, :],
                                     ident[:, :], start=True, stop=True)
                    if b % 4 == 3:
                        last.then_inc(s_gar_ps, 1)

            def step(b, own, prev, nxt):
                for h in range(H):
                    n = b * H + h
                    if own:
                        g, j = h // HT, h % HT
                        if j == 0:
                            pe.wait_ge(s_rep, QUADS * b + g + 1)
                        at_least(pe, s_z, n - 1)
                        for qt in range(QT):
                            part = stack[32 * j:32 * (j + 1), g, :, :]
                            last = pe.matmul(score_bank[h % 2][:, qt * S:(qt + 1) * S],
                                             part[:, 0, qt * P:(qt + 1) * P], part[:, 1, :], start=True, stop=True)
                        last.then_inc(s_score, 1)
                    if (own and h >= 3) or (prev and h < 3):
                        m = b * H + h - 3
                        slot = (h - 3) % ZR
                        if isinstance(b, int) and b == 0 and h == 3:
                            pe.wait_ge(s_gar, 4)
                        pe.wait_ge(s_w_sub, m + 1)
                        at_least(pe, s_p, m - 1)
                        for qt in range(QT):
                            for kt in range(QT):
                                at = kt * S + qt * P
                                last = turn(turned_bank[(h - 3) % 2][:, at:at + P],
                                            w[:, slot, qt, kt * P:(kt + 1) * P])
                        last.then_inc(s_t, 1)
                    if (prev and h == 3) or (own and h in (7, 11, 15)):
                        quad = b * QUADS + (h - 7) // 4
                        g = ((h - 7) // 4) % QUADS
                        pe.wait_ge(s_p, HT * (quad + 1))
                        at_least(pe, s_o, quad)
                        if h == 7:
                            pe.wait_ge(s_v, b + 1)
                        for kt in range(QT):
                            for j in range(HT):
                                last = pe.matmul(pv_bank[32 * j:32 * (j + 1), 0:S], v_wide[:, kt, HT * g + j, :],
                                                 probs[:, (HT * g + j) % PR, kt, :], start=(kt == 0),
                                                 stop=(kt == QT - 1), skip_group_check=True)
                        last.then_inc(s_pv, 1)
                    if (prev and h in (0, 4)) or (own and h in (8, 12)):
                        quad = b * QUADS + h // 4 - 2
                        pe.wait_ge(s_o, quad + 1)
                        at_least(pe, s_at, quad)
                        for qt in range(QT):
                            last = turn(ot_bank[:, qt * P:(qt + 1) * P], o_sb[:, qt * P:(qt + 1) * P])
                        last.then_inc(s_oT, 1)
                    if own and h == 1:
                        make_stack(b, QUADS - 1)
                    if own and h == 4:
                        pe.wait_ge(s_rep, QUADS * (b + 1))
                        for qt in range(QT):
                            last = pe.matmul(front_bank[:, qt * D:(qt + 1) * D], h_t[:, qt * P:(qt + 1) * P],
                                             w_t[:, 2, :], start=True, stop=True)
                        last.then_inc(s_v_ps, 1)
                    if nxt and h == 6:
                        turn_normed(b + 1)
                    if prev and h == 6:
                        pe.wait_ge(s_at, QUADS * b)
                        at_least(pe, s_w2l, b)
                        for qt in range(QT):
                            last = turn(tail_bank[:, qt * P:(qt + 1) * P], attn[:, qt, :])
                        last.then_inc(s_aT_ps, 1)
                    if prev and h == 7:
                        pe.wait_ge(s_aT, b)
                        for qt in range(QT):
                            last = pe.matmul(tail_bank[:, S + qt * D:S + (qt + 1) * D],
                                             attn_t[:, qt * P:(qt + 1) * P], w_t[:, 3, :], start=True, stop=True)
                        last.then_inc(s_y, 1)
                    if nxt and h == 8:
                        project_qk(b + 1)
                    if own and h == 9:
                        pe.wait_ge(s_ws, 2 * b + 1)
                        at_least(pe, s_yg, b)
                        for k in range(HC):
                            last = turn(tail_bank[:, k * P:(k + 1) * P], w1_scaled[:, k, :])
                        last.then_inc(s_w1T, 1)
                    if nxt and h in (11, 12, 13):
                        make_stack(b + 1, h - 11)
                    if own and h == 13:
                        pe.wait_ge(s_ws, 2 * b + 2)
                        pe.wait_ge(s_w1l, b + 1)
                        for k in range(HC):
                            last = turn(tail_bank[:, k * P:(k + 1) * P], w2_scaled[:, k * P:(k + 1) * P])
                        last.then_inc(s_w2T, 1)

            batches(pe, step)

            def front_turn(g):
                pe.wait_ge(s_norm2, g + 1)
                at_least(pe, s_h2, g)
                for t in range(GT):
                    last = turn(bank[5][:, t * P:(t + 1) * P], normed2[:, t, :])
                last.then_inc(s_h2_ps, 1)

            def front_logits(g):
                pe.wait_ge(s_h2, g + 1)
                pe.wait_ge(s_gate, 1)
                at_least(pe, s_mask, g)
                for t in range(GT):
                    last = pe.matmul(bank[7][:, t * E:(t + 1) * E], h2_t[:, t * P:(t + 1) * P], gate_t[:, :],
                                     start=True, stop=True)
                last.then_inc(s_logit_ps, 1)

            def front_mask(g):
                pe.wait_ge(s_chosen, 2 * g + 2)
                for t in range(GT):
                    last = turn(bank[7][0:E, t * P:(t + 1) * P], chosen[:, 2, t, :])
                last.then_inc(s_mask_ps, 1)

            def first_product(g, t):
                e, k = t // HC, t % HC
                no = N1 * g + t
                if t == 0:
                    pe.wait_ge(s_xlo, g + 1)
                at_least(pe, s_silu, no - 1)
                part = slice(k * P, (k + 1) * P)
                for i, (weights, tokens) in enumerate(((w1_hi, x_hi), (w1_hi, x_lo), (w1_lo, x_hi))):
                    last = pe.matmul(bank[t % 2][:, :], weights[:, e, part], tokens[:, bass.ds(g, 1), :],
                                     start=(i == 0), stop=(i == 2))
                last.then_inc(s_l1, 1)

            def second_product(g, t):
                e, k = t // HC, t % HC
                if k == 0:
                    at_least(pe, s_masked, E * g + e - 1)
                pe.wait_ge(s_hlo, N1 * g + t + 1)
                hi, lo = h_hi[t % 2], h_lo[:, t % 2, :]
                for i, (weights, part) in enumerate(((w2_hi, hi), (w2_hi, lo), (w2_lo, hi))):
                    last = pe.matmul(bank[2 + e % 2][:, :], weights[:, e, k, :], part,
                                     start=(k == 0 and i == 0), stop=(k == HC - 1 and i == 2))
                last.then_inc(s_l2, 1)

            def expert_step(g, own, prev, nxt):
                for t in range(N1):
                    if own:
                        first_product(g, t)
                    if own and t >= 2:
                        second_product(g, t - 2)
                    if prev and t < 2:
                        second_product(g - 1, N1 + t - 2)
                    if own and t % HC == 0:
                        e = t // HC
                        if e == 0:
                            pe.wait_ge(s_mask, g + 1)
                        copied = counted(pe, E * g + e)
                        pe.wait_ge(s_choose, 1)
                        at_least(pe, s_wide, copied)
                        pe.matmul(bank[4][:, :], choose[:, e, :], mask_t[:, bass.ds(g, 1), :], start=True,
                                  stop=True).then_inc(s_wide_ps, 1)
                    if prev and t == 5:
                        pe.wait_ge(s_gated2, g)
                        at_least(pe, s_final, g - 1)
                        for i in range(GT):
                            last = turn(bank[6][:, i * P:(i + 1) * P], gated2[:, i * P:(i + 1) * P])
                        last.then_inc(s_back, 1)
                    if nxt and t == 15:
                        front_turn(g + 1)
                    if nxt and t == 17:
                        front_logits(g + 1)
                    if nxt and t == 27:
                        front_mask(g + 1)

            pe.wait_ge(s_gsq, 4)
            pe.wait_ge(s_yg, B)
            turn(bank[7][:, 0:E], gate_scaled[:, :], E).then_inc(s_gate_ps, 1)
            front_turn(0)
            front_logits(0)
            front_mask(0)
            groups(pe, expert_step)


_INS = ['L0_attn_x', 'L0_attn_Wq', 'L0_attn_bq', 'L0_attn_Wk', 'L0_attn_bk', 'L0_attn_Wv', 'L0_attn_bv',
        'L0_attn_Wo', 'L0_attn_bo', 'L0_attn_rel_bias', 'L0_ffn_gate_v', 'L0_ffn_gate_g', 'L0_ffn_gate_b',
        'L0_ffn_w1_v', 'L0_ffn_w1_g', 'L0_ffn_b1', 'L0_ffn_w2_v', 'L0_ffn_w2_g', 'L0_ffn_b2', 'L0_c', 'L0_wmod']


def kernel(**inputs):
    import numpy as _np
    import concourse.bacc as _bacc
    from concourse import mybir as _mybir
    from concourse.bass_utils import run_bass_kernel_spmd as _run

    nc = _bacc.Bacc("TRN2", target_bir_lowering=False, num_devices=1)
    arrays, args = {}, []
    for name in _INS:
        a = _np.ascontiguousarray(inputs[name])
        if name == 'L0_attn_rel_bias':
            S = inputs['L0_attn_x'].shape[1]
            reach = (a.shape[1] - 1) // 2
            at = _np.clip(_np.arange(2 * S) - (S - 1), -reach, reach) + reach
            a = _np.ascontiguousarray(a[:, at])
        arrays[f"in_{name}_dram"] = a
        args.append(nc.dram_tensor(f"in_{name}_dram", a.shape, _mybir.dt.from_np(a.dtype), kind="ExternalInput").ap())
    out = nc.dram_tensor("out_0_dram", inputs['L0_attn_x'].shape, _mybir.dt.float32, kind="ExternalOutput").ap()
    adaln_block_kernel(nc, *args, out)
    r = _run(nc, [arrays], core_ids=[0])
    return r.results[0]["out_0_dram"]
```

```python
from contextlib import ExitStack

import concourse.bass as bass
from concourse import mybir

F32 = mybir.dt.float32
F32R = mybir.dt.float32r
BF16 = mybir.dt.bfloat16
U32 = mybir.dt.uint32
ALU = mybir.AluOpType
ACT = mybir.ActivationFunctionType
AX = mybir.AxisListType

P = 128
LN_EPS = 1e-5
NORM_EPS = 1e-12
GATE_FLOOR = 0.25
LOG_SMALLEST = -104.0


def at_least(engine, semaphore, count):
    if not isinstance(count, int) or count > 0:
        engine.wait_ge(semaphore, count)


def counted(engine, count):
    if not isinstance(count, int):
        engine.compute_val(count)
    return count


def column_places(B, E, HC):
    places, at = {}, 0
    for name, n in (("c", B), ("bq", 1), ("bk", 1), ("bv", 1), ("bo", 1), ("b1", E * HC), ("w1_g", E * HC),
                    ("w2_g", E), ("b2", E)):
        places[name] = at
        at += n
    return places, at


def adaln_block_kernel(nc, x, w_in_out, columns, rel_ext, gate_v, gate_g, gate_b, w1_v, w2_v, wmod, out):
    B, S, D = x.shape
    H = rel_ext.shape[0]
    DK = D // H
    E, HID, _ = w1_v.shape
    QT = S // P
    TILES = B * QT
    HT = 4
    QUADS = H // HT
    REP = P // (HT * DK)
    HC = HID // P
    GROUP = 512
    GT = GROUP // P
    GB = GROUP // S
    GROUPS = B * S // GROUP
    BW = S + P
    SCORE_SCALE = float(DK) ** -0.5
    assert D == P and S == 2 * P and HT * DK * REP == P and B == E and E == 8

    places, COLS = column_places(B, E, HC)
    C_C, C_BQ, C_BK, C_BV, C_BO = (places[name] for name in ("c", "bq", "bk", "bv", "bo"))
    C_B1, C_W1G, C_W2G, C_B2 = (places[name] for name in ("b1", "w1_g", "w2_g", "b2"))

    with ExitStack() as ctx:
        def sb(name, shape, dt=F32):
            return ctx.enter_context(nc.sbuf_tensor(name, shape, dt))

        def sem(name):
            return ctx.enter_context(nc.semaphore(name))

        bank = [ctx.enter_context(nc.psum_tensor(f"bank{i}", [P, 512], F32)) for i in range(8)]
        score_bank, turned_bank = bank[0:2], bank[2:4]
        pv_bank, ot_bank, front_bank, tail_bank = bank[4:8]

        ident = sb("ident", [P, P])
        sel = sb("sel", [P, 4, QUADS, HT, REP, DK], F32R)
        w_t = sb("w_t", [P, 4, D])
        cols = sb("cols", [P, COLS])
        bq_scaled = sb("bq_scaled", [P, 1])
        silu_c = sb("silu_c", [P, 3, B])
        wmod_sb = sb("wmod_sb", [P, 6 * D])
        mod = sb("mod", [P, 6, B])
        gate_tmp = sb("gate_tmp", [P, 2, 2, B])
        ga_col = sb("ga_col", [P, 2, B])
        gb_col = sb("gb_col", [P, B])
        band = sb("band", [P, H, BW])

        x_sb = sb("x_sb", [P, TILES, D])
        stats = sb("stats", [P, TILES, 6])
        mean_var = sb("mean_var", [P, TILES, 2])
        rstd = sb("rstd", [P, TILES])
        minus_half = sb("minus_half", [P, TILES])
        half = sb("half", [P, 8])

        normed = sb("normed", [P, QT, D])
        h_t = sb("h_t", [P, S])
        qk = sb("qk", [P, 2, S])
        qk_hi = sb("qk_hi", [P, 2, S], F32R)
        qk_lo = sb("qk_lo", [P, 2, S], F32R)
        stack = sb("stack", [P, QUADS, 2, S], F32R)
        v_wide = sb("v_wide", [P, QT, H, 32])
        ZR = 4
        z = sb("z", [P, ZR, QT, S])
        z_max = sb("z_max", [P, ZR, QT])
        w = sb("w", [P, ZR, QT, S])
        PR = 8
        probs = sb("probs", [P, PR, QT, S])
        o_sb = sb("o_sb", [P, S])
        recip = sb("recip", [P, QT, HT])
        attn = sb("attn", [P, QT, D])
        attn_t = sb("attn_t", [P, S])
        gated_t = sb("gated_t", [P, S])

        w1_raw = sb("w1_raw", [P, HC, D])
        w2_raw = sb("w2_raw", [P, HID])
        squares = sb("squares", [P, HID])
        norm_sq = sb("norm_sq", [P, 8])
        norm = sb("norm", [P, 8])
        norm_scale = sb("norm_scale", [P, 3, 8])
        w1_scaled = sb("w1_scaled", [P, HC, D])
        w2_scaled = sb("w2_scaled", [P, HID])
        w1_hi = sb("w1_hi", [P, E, HID], F32R)
        w1_lo = sb("w1_lo", [P, E, HID], F32R)
        w2_hi = sb("w2_hi", [P, E, HC, D], F32R)
        w2_lo = sb("w2_lo", [P, E, HC, D], F32R)

        gate_rows = sb("gate_rows", [E, D])
        gate_g_col = sb("gate_g_col", [E, 1])
        gate_b_row = sb("gate_b_row", [P, E])
        gate_sq = sb("gate_sq", [E, D])
        gate_norm = sb("gate_norm", [E, 4])
        gate_scaled = sb("gate_scaled", [E, D])
        gate_t = sb("gate_t", [P, E])
        stats2 = sb("stats2", [P, GT, 6])
        mean_var2 = sb("mean_var2", [P, GT, 2])
        rstd2 = sb("rstd2", [P, GT])
        choose = sb("choose", [E, E, P], BF16)
        expert_no = sb("expert_no", [P, GT, E])
        logits = sb("logits", [P, 3, GT, E])
        top = sb("top", [P, GT])
        top8 = sb("top8", [P, GT, 8])
        top_at = sb("top_at", [P, GT, 8], U32)
        top_no = sb("top_no", [P, GT, 2])
        chosen = sb("chosen", [P, 3, GT, E])
        mask_t = sb("mask_t", [E, GROUPS, GROUP], BF16)
        x_hi = stack[:, :, :, :].rearrange("p g i s -> p g (i s)")
        x_lo = sel[:, :, :, :, :, :].rearrange("p k g j r d -> p k (g j r d)")
        HR = 4
        hidden = z[:, :, :, :].rearrange("p i t s -> p i (t s)")
        h_lo = sb("h_lo", [P, HR, GROUP], F32R)
        h_hi_rest = sb("h_hi_rest", [P, HR - 2, GROUP], F32R)
        h_hi = [part[:, :, :].rearrange("p i s -> p (i s)") for part in (qk_hi, qk_lo)] + [
            h_hi_rest[:, i, :] for i in range(HR - 2)]
        normed2 = squares[:, :].rearrange("p (t d) -> p t d", t=GT)
        h2_t = w1_raw[:, :, :].rearrange("p k d -> p (k d)")
        spare = band[:, :, :].rearrange("p h u -> p (h u)").rearrange("p (i n) -> p i n", n=GROUP)
        mask_wide, masked = spare[:, 0:2, :], spare[:, 2:4, :]
        summed, gated2 = spare[:, 4, :], spare[:, 5, :]

        s_x = [sem(f"x_loaded{i}") for i in range(2)]
        s_cols = sem("columns_loaded")
        s_bq = sem("bq_scaled_done")
        s_w = sem("weights_loaded")
        s_wmod = sem("wmod_loaded")
        s_band = [sem(f"band_loaded{i}") for i in range(QUADS)]
        s_exp_w = sem("expert_weights_loaded")
        s_ident0 = sem("ident_zeroed")
        s_ident = sem("ident_ready")
        s_consts = sem("pool_constants_ready")
        s_selz = sem("sel_zeroed")
        s_sel = sem("sel_ready")
        s_vz = sem("v_wide_zeroed")
        s_vinit = sem("v_wide_ready")
        s_cexp = sem("c_exp_done")
        s_sc = sem("silu_c_step")
        s_mod_ps = sem("mod_in_psum")
        s_mod = sem("mod_step")
        s_stats = sem("stats_done")
        s_mv = sem("mean_var_done")
        s_eps = sem("eps_added")
        s_rstd = sem("rstd_done")

        s_norm = sem("normed_ready")
        s_hT_ps = sem("h_t_in_psum")
        s_hT = sem("h_t_ready")
        s_qk_ps = sem("qk_in_psum")
        s_qk = sem("qk_ready")
        s_hi = sem("qk_hi_ready")
        s_lo = sem("qk_lo_ready")
        s_rep_ps = sem("stack_in_psum")
        s_rep = sem("stack_ready")
        s_v_ps = sem("v_in_psum")
        s_v = sem("v_ready")
        s_score = sem("score_done")
        s_z = sem("z_ready")
        s_w_sub = sem("w_ready")
        s_t = sem("w_turned")
        s_p = sem("probs_ready")
        s_pv = sem("pv_done")
        s_o = sem("o_evacuated")
        s_oT = sem("o_turned")
        s_rc = sem("recip_done")
        s_at = sem("attn_ready")
        s_aT_ps = sem("attn_turned")
        s_aT = sem("attn_t_ready")
        s_y = sem("y_done")
        s_yg = sem("gated_t_ready")
        s_yb = sem("gated_turned")
        s_x2 = sem("x2_ready")

        s_sq = sem("squares_done")
        s_nrm = sem("norm_done")
        s_ns = sem("norm_scale_step")
        s_ws = sem("w_scaled")
        s_w1T = sem("w1_turned")
        s_w2T = sem("w2_turned")
        s_w1h = sem("w1_hi_done")
        s_w2h = sem("w2_hi_done")
        s_w1l = sem("w1_lo_done")
        s_w2l = sem("w2_lo_done")
        s_out = sem("out_stored")

        s_gate_in = sem("gate_inputs_loaded")
        s_gsq = sem("gate_prep_step")
        s_gnorm = sem("gate_norm_done")
        s_gate_ps = sem("gate_t_in_psum")
        s_gate = sem("gate_t_ready")
        s_no = sem("expert_numbers_ready")
        s_choose = sem("choose_ready")
        s_stats2 = sem("stats2_done")
        s_eps2 = sem("eps2_step")
        s_rstd2 = sem("rstd2_done")
        s_norm2 = sem("normed2_ready")
        s_h2_ps = sem("h2_in_psum")
        s_h2 = sem("h2_ready")
        s_xhi = sem("x_hi_ready")
        s_xlo = sem("x_lo_ready")
        s_logit_ps = sem("logits_in_psum")
        s_logit = sem("logits_step")
        s_top = sem("top_step")
        s_chosen = sem("chosen_step")
        s_mask_ps = sem("mask_t_in_psum")
        s_mask = sem("mask_t_ready")
        s_wide_ps = sem("mask_wide_in_psum")
        s_wide = sem("mask_wide_ready")
        s_l1 = sem("hidden_in_psum")
        s_silu = sem("hidden_ready")
        s_hhi = [sem(f"h_hi_ready_{by}") for by in ("dve", "act")]
        s_hlo = sem("h_lo_ready")
        s_l2 = sem("l2_done")
        s_masked = sem("masked_ready")
        s_sum = sem("summed_step")
        s_gated2 = sem("gated2_ready")
        s_back = sem("gated2_turned")
        s_final = sem("final_ready")

        block = ctx.enter_context(nc.Block())
        x_dram = x.rearrange("b (t p) d -> p (b t) d", p=P)
        w1_dram = w1_v.rearrange("e (k p) d -> p (e k) d", p=P)
        w2_dram = w2_v.rearrange("e d h -> d e h")
        out_dram = out.rearrange("b (t p) d -> p (b t) d", p=P)

        def band_dram(g):
            width = rel_ext.shape[1]
            return bass.AP(rel_ext.tensor, HT * g * width, [[1, P], [width, HT], [1, BW]])

        CLOSING = 3

        def batches(engine, head_step):
            for h in range(H):
                head_step(0, h, True, False, True)
            with engine.Fori(1, B - 1) as b:
                for h in range(H):
                    head_step(b, h, True, True, True)
            for h in range(H):
                head_step(B - 1, h, True, True, False)
            for h in range(CLOSING):
                head_step(B, h, False, True, False)

        N1 = E * HC
        LAG = 3

        def groups(engine, step):
            step(0, True, False, True)
            with engine.Fori(1, GROUPS - 1) as g:
                step(g, True, True, True)
            step(GROUPS - 1, True, True, False)
            step(GROUPS, False, True, False)

        @block.sync
        def _(sp):
            sp.dma_start(cols[:, :], columns).then_inc(s_cols, 16)
            sp.dma_start(x_sb[:, 0:QT, :], x_dram[:, 0:QT, :]).then_inc(s_x[0], 16)
            sp.dma_start(wmod_sb[:, :], wmod).then_inc(s_wmod, 16)
            sp.dma_start(w_t[:, :, :], w_in_out).then_inc(s_w, 16)
            sp.dma_start(x_sb[:, QT:TILES, :], x_dram[:, QT:TILES, :]).then_inc(s_x[1], 16)
            for g in range(QUADS):
                sp.dma_start(band[:, HT * g:HT * (g + 1), :], band_dram(g)).then_inc(s_band[g], 16)

            def load_expert(e):
                sp.dma_start(w1_raw[:, :, :], w1_dram[:, bass.ds(e * HC, HC), :]).then_inc(s_exp_w, 16)
                sp.dma_start(w2_raw[:, :], w2_dram[:, bass.ds(e, 1), :]).then_inc(s_exp_w, 16)

            load_expert(0)
            with sp.Fori(1, E) as e:
                sp.wait_ge(s_ws, 2 * e)
                load_expert(e)
            sp.wait_ge(s_final, 1)
            sp.dma_start(out_dram[:, 0:GT, :], x_sb[:, 0:GT, :]).then_inc(s_out, 16)
            with sp.Fori(1, GROUPS) as g:
                sp.wait_ge(s_final, g + 1)
                sp.dma_start(out_dram[:, bass.ds(g * GT, GT), :],
                             x_sb[:, bass.ds(g * GT, GT), :]).then_inc(s_out, 16)
            sp.wait_ge(s_out, 16 * GROUPS)

        @block.gpsimd
        def _(pool):
            pool.memset(ident[:, :], 0.0).then_inc(s_ident0, 1)
            pool.memset(minus_half[:, :], -0.5).then_inc(s_consts, 1)
            pool.memset(half[:, :], 0.5).then_inc(s_consts, 1)
            pool.wait_ge(s_ident0, 1)
            pool.affine_select(out=ident[:, :], in_=ident[:, :], compare_op=ALU.not_equal, fill=1.0, base=0,
                               pattern=[[-1, P]], channel_multiplier=1).then_inc(s_ident, 1)
            pool.wait_ge(s_consts, 2)
            for i, (a, e) in enumerate(((0, QT), (QT, TILES))):
                if i == 1:
                    pool.memset(sel[:, :, :, :, :, :].bitcast(F32), 0.0).then_inc(s_selz, 1)
                    pool.wait_ge(s_selz, 1)
                    pool.wait_ge(s_ident, 1)
                    ones = ident[:, :].rearrange("p (g j d) -> p g j d", g=QUADS, j=HT)
                    for k, reps in enumerate(((0, 1), (2, 3), (0, 2), (1, 3))):
                        for r in reps:
                            pool.tensor_copy(sel[:, k, :, :, r, :], ones).then_inc(s_sel, 1)
                    pool.memset(v_wide[:, :, :, :], 0.0).then_inc(s_vz, 1)
                    pool.wait_ge(s_vz, 1)
                    pool.memset(v_wide[:, :, :, DK:DK + 1], 1.0).then_inc(s_vinit, 1)
                    pool.iota(expert_no[:, :, :], pattern=[[0, GT], [1, E]], base=0, channel_multiplier=0,
                              allow_small_or_imprecise_dtypes=True).then_inc(s_no, 1)
                    pool.tensor_copy(choose[:, :, :], ident[0:E, 0:E].unsqueeze(2).to_broadcast([E, E, P])).then_inc(s_choose, 1)
                pool.wait_ge(s_eps, i + 1)
                pool.tensor_tensor(rstd[:, a:e], mean_var[:, a:e, 1], minus_half[:, a:e],
                                   ALU.pow).then_inc(s_rstd, 1)
            pool.wait_ge(s_gsq, 1)
            pool.tensor_tensor(gate_norm[:, 1:2], gate_norm[:, 0:1], half[0:E, 0:1], ALU.pow).then_inc(s_gnorm, 1)

            def front(g):
                pool.wait_ge(s_eps2, 2 * g + 2)
                pool.tensor_tensor(rstd2[:, :], mean_var2[:, :, 1], minus_half[:, 0:GT], ALU.pow).then_inc(s_rstd2, 1)

            def head_step(b, h, own, prev, nxt):
                if not own:
                    return
                n = b * H + h
                ready, turned = counted(pool, n + 1), counted(pool, n - ZR + 1)
                pool.wait_ge(s_consts, 2)
                pool.wait_ge(s_z, ready)
                at_least(pool, s_t, turned)
                for qt in range(QT):
                    sub = pool.tensor_scalar(w[:, h % ZR, qt, :], z[:, h % ZR, qt, :], -1.0,
                                             z_max[:, h % ZR, qt:qt + 1], ALU.mult, ALU.add)
                sub.then_inc(s_w_sub, 1)
                if h == 5:
                    pool.wait_ge(s_sq, (b + 1) * (HC + 1))
                    at_least(pool, s_ns, 3 * b)
                    pool.tensor_tensor(norm[:, 0:HC + 1], norm_sq[:, 0:HC + 1], half[:, 0:HC + 1],
                                       ALU.pow).then_inc(s_nrm, 1)
                if not nxt and h == 4:
                    front(0)

            batches(pool, head_step)

            def expert_step(g, own, prev, nxt):
                if prev:
                    e = E - 1
                    done = (E - 1) * (g - 1)
                    pool.wait_ge(s_masked, E * g)
                    pool.wait_ge(s_sum, done + e - 1)
                    pool.tensor_tensor(summed, summed, masked[:, e % 2, :], ALU.add).then_inc(s_sum, 1)
                if not own:
                    return
                for e in range(1, E - 1):
                    done = (E - 1) * g
                    pool.wait_ge(s_masked, E * g + e + 1)
                    at_least(pool, s_sum, done + e - 1)
                    pool.tensor_tensor(summed, summed, masked[:, e % 2, :], ALU.add).then_inc(s_sum, 1)
                    if nxt and e == 1:
                        front(g + 1)

            groups(pool, expert_step)

        @block.vector
        def _(dve):
            def norm_stats(a, e):
                for t in range(a, e):
                    dve.bn_stats(stats[:, t, :], x_sb[:, t, :]).then_inc(s_stats, 1)
                dve.wait_ge(s_stats, e)
                for t in range(a, e):
                    dve.bn_aggr(mean_var[:, t, :], stats[:, t, :]).then_inc(s_mv, 1)
                dve.wait_ge(s_mv, e)
                dve.tensor_scalar(mean_var[:, a:e, 1], mean_var[:, a:e, 1], LN_EPS, None,
                                  ALU.add).then_inc(s_eps, 1)

            def make_normed(b):
                at_least(dve, s_hT_ps, b)
                for qt in range(QT):
                    t = b * QT + qt
                    last = dve.tensor_scalar(normed[:, qt, :], x_sb[:, bass.ds(t, 1), :],
                                             mean_var[:, bass.ds(t, 1), 0], rstd[:, bass.ds(t, 1)],
                                             ALU.subtract, ALU.mult)
                last.then_inc(s_norm, 1)

            def make_h_t(b):
                dve.wait_ge(s_hT_ps, b + 1)
                at_least(dve, s_v_ps, b)
                dve.tensor_scalar(h_t[:, :], front_bank[:, 0:S], mod[:, 1, bass.ds(b, 1)],
                                  mod[:, 0, bass.ds(b, 1)], ALU.mult, ALU.add).then_inc(s_hT, 1)

            def split_hi(b):
                dve.wait_ge(s_qk, 2 * (b + 1))
                at_least(dve, s_rep_ps, QUADS * b)
                dve.tensor_copy(qk_hi[:, :, :], qk[:, :, :]).then_inc(s_hi, 1)

            def split_lo(b):
                dve.wait_ge(s_hi, b + 1)
                dve.tensor_tensor(qk_lo[:, :, :], qk[:, :, :], qk_hi[:, :, :].bitcast(F32),
                                  ALU.subtract).then_inc(s_lo, 1)

            dve.wait_ge(s_x[0], 16)
            norm_stats(0, QT)
            dve.wait_ge(s_cols, 16)
            dve.tensor_scalar(bq_scaled[:, :], cols[:, C_BQ:C_BQ + 1], SCORE_SCALE, None, ALU.mult).then_inc(s_bq, 1)
            dve.wait_ge(s_cexp, 1)
            dve.tensor_scalar(silu_c[:, 1, :], silu_c[:, 0, :], 1.0, None, ALU.add).then_inc(s_sc, 1)
            dve.wait_ge(s_sc, 1)
            dve.reciprocal(silu_c[:, 2, :], silu_c[:, 1, :]).then_inc(s_sc, 1)
            dve.wait_ge(s_sc, 2)
            dve.tensor_tensor(silu_c[:, 0, :], silu_c[:, 2, :], cols[:, C_C:C_C + B], ALU.mult).then_inc(s_sc, 1)
            dve.wait_ge(s_rstd, 1)
            make_normed(0)
            dve.wait_ge(s_mod_ps, 1)
            dve.tensor_copy(mod[:, :, :], bank[2][:, 0:6 * B].rearrange("p (j b) -> p j b", j=6)).then_inc(s_mod, 1)
            dve.wait_ge(s_mod, 1)
            for j in (1, 4):
                dve.tensor_scalar(mod[:, j, :], mod[:, j, :], 1.0, None, ALU.add).then_inc(s_mod, 1)
            dve.wait_ge(s_mod, 3)
            make_h_t(0)
            for i, j in enumerate((2, 5)):
                g = mod[:, j, :]
                dve.tensor_scalar(gate_tmp[:, i, 0, :], g, 0.0, 2.0, ALU.is_ge, ALU.mult).then_inc(s_mod, 1)
                dve.scalar_tensor_tensor(out=gate_tmp[:, i, 1, :], in0=g, scalar=-1.0, in1=g, op0=ALU.mult,
                                         op1=ALU.max).then_inc(s_mod, 1)
            dve.wait_ge(s_mod, 7)
            for i in range(2):
                dve.tensor_scalar(gate_tmp[:, i, 1, :], gate_tmp[:, i, 1, :], GATE_FLOOR, None,
                                  ALU.max).then_inc(s_mod, 1)
            dve.wait_ge(s_mod, 9)
            for i, o in enumerate((ga_col[:, 0, :], gb_col[:, :])):
                dve.scalar_tensor_tensor(out=o, in0=gate_tmp[:, i, 0, :], scalar=-1.0, in1=gate_tmp[:, i, 1, :],
                                         op0=ALU.add, op1=ALU.mult).then_inc(s_mod, 1)
            split_hi(0)
            dve.wait_ge(s_mod, 11)
            dve.tensor_scalar(ga_col[:, 1, :], ga_col[:, 0, :], cols[:, C_BO:C_BO + 1], None,
                              ALU.mult).then_inc(s_mod, 1)
            split_lo(0)
            dve.wait_ge(s_x[1], 16)
            norm_stats(QT, TILES)
            dve.wait_ge(s_gate_in, 48)
            dve.tensor_tensor_reduce(gate_sq[:, :], gate_rows[:, :], gate_rows[:, :], 1.0, 0.0, ALU.mult, ALU.add,
                                     gate_norm[:, 0:1]).then_inc(s_gsq, 1)
            dve.wait_ge(s_gnorm, 1)
            dve.tensor_scalar(gate_norm[:, 2:3], gate_norm[:, 1:2], NORM_EPS, None, ALU.max).then_inc(s_gsq, 1)
            dve.wait_ge(s_gsq, 2)
            dve.reciprocal(gate_norm[:, 3:4], gate_norm[:, 2:3]).then_inc(s_gsq, 1)
            dve.wait_ge(s_gsq, 3)
            dve.tensor_scalar(gate_scaled[:, :], gate_rows[:, :], gate_norm[:, 3:4], gate_g_col[:, 0:1], ALU.mult,
                              ALU.mult).then_inc(s_gsq, 1)

            def front_stats(g):
                for t in range(GT):
                    last = dve.bn_stats(stats2[:, t, :], x_sb[:, bass.ds(g * GT + t, 1), :])
                last.then_inc(s_stats2, 1)

            def front_mean_var(g):
                seen = counted(dve, g + 1)
                dve.wait_ge(s_no, 1)
                dve.wait_ge(s_stats2, seen)
                for t in range(GT):
                    last = dve.bn_aggr(mean_var2[:, t, :], stats2[:, t, :])
                last.then_inc(s_eps2, 1)
                dve.wait_ge(s_eps2, 2 * g + 1)
                dve.tensor_scalar(mean_var2[:, :, 1], mean_var2[:, :, 1], LN_EPS, None, ALU.add).then_inc(s_eps2, 1)

            def front_normed(g):
                dve.wait_ge(s_rstd2, g + 1)
                at_least(dve, s_h2_ps, g)
                for t in range(GT):
                    last = dve.tensor_scalar(normed2[:, t, :], x_sb[:, bass.ds(g * GT + t, 1), :],
                                             mean_var2[:, t, 0:1], rstd2[:, t:t + 1], ALU.subtract, ALU.mult)
                last.then_inc(s_norm2, 1)

            def front_h2(g):
                dve.wait_ge(s_h2_ps, g + 1)
                at_least(dve, s_logit_ps, g)
                for i in range(GB):
                    b = bass.ds(g * GB + i, 1)
                    last = dve.tensor_scalar(h2_t[:, i * S:(i + 1) * S], front_bank[:, i * S:(i + 1) * S], mod[:, 4, b],
                                             mod[:, 3, b], ALU.mult, ALU.add)
                last.then_inc(s_h2, 1)

            def front_lo(g):
                dve.wait_ge(s_xhi, g + 1)
                dve.tensor_tensor(x_lo[:, bass.ds(g, 1), :], h2_t[:, :].unsqueeze(1),
                                  x_hi[:, bass.ds(g, 1), :].bitcast(F32), ALU.subtract).then_inc(s_xlo, 1)

            def front_gates(g, part):
                wide = [P, GT, E]
                if part == 0:
                    dve.wait_ge(s_logit_ps, g + 1)
                    dve.tensor_tensor(logits[:, 0, :, :], front_bank[:, 0:GT * E].rearrange("p (t e) -> p t e", t=GT),
                                      gate_b_row[:, :].unsqueeze(1).to_broadcast(wide), ALU.add).then_inc(s_logit, 1)
                    dve.wait_ge(s_logit, 4 * g + 1)
                    dve.tensor_reduce(top[:, :], logits[:, 0, :, :], AX.X, ALU.max).then_inc(s_logit, 1)
                    dve.wait_ge(s_logit, 4 * g + 2)
                    dve.tensor_tensor(logits[:, 1, :, :], logits[:, 0, :, :],
                                      top[:, :].unsqueeze(2).to_broadcast(wide), ALU.subtract).then_inc(s_logit, 1)
                    dve.wait_ge(s_logit, 4 * g + 3)
                    dve.tensor_scalar(logits[:, 2, :, :], logits[:, 1, :, :], LOG_SMALLEST, None,
                                      ALU.max).then_inc(s_logit, 1)
                if part == 1:
                    seen = counted(dve, 4 * g + 4)
                    dve.wait_ge(s_no, 1)
                    dve.wait_ge(s_logit, seen)
                    for t in range(GT):
                        last = dve.max(top8[:, t, :], logits[:, 2, t, :])
                    last.then_inc(s_top, 1)
                    seen = counted(dve, 3 * g + 1)
                    dve.wait_ge(s_no, 1)
                    dve.wait_ge(s_top, seen)
                    for t in range(GT):
                        last = dve.max_index(top_at[:, t, :], top8[:, t, :], logits[:, 2, t, :])
                    last.then_inc(s_top, 1)
                    dve.wait_ge(s_top, 3 * g + 2)
                    dve.tensor_copy(top_no[:, :, :], top_at[:, :, 0:2]).then_inc(s_top, 1)
                if part == 2:
                    dve.wait_ge(s_top, 3 * g + 3)
                    at_least(dve, s_mask_ps, g)
                    for k in range(2):
                        last = dve.tensor_tensor(chosen[:, k, :, :], expert_no[:, :, :],
                                                 top_no[:, :, k].unsqueeze(2).to_broadcast(wide), ALU.is_equal)
                    last.then_inc(s_chosen, 1)
                    dve.wait_ge(s_chosen, 2 * g + 1)
                    dve.tensor_tensor(chosen[:, 2, :, :], chosen[:, 0, :, :], chosen[:, 1, :, :],
                                      ALU.add).then_inc(s_chosen, 1)

            def head_step(b, h, own, prev, nxt):
                n = b * H + h
                if own:
                    scored, subtracted = counted(dve, n + 1), counted(dve, n - ZR + 1)
                    dve.wait_ge(s_band[h // HT], 16)
                    dve.wait_ge(s_score, scored)
                    at_least(dve, s_w_sub, subtracted)
                    for qt in range(QT):
                        last_key = qt * P
                        last = dve.tensor_tensor_reduce(
                            z[:, h % ZR, qt, :], score_bank[h % 2][:, qt * S:(qt + 1) * S],
                            band[:, h, last_key:last_key + S][:, ::-1], 1.0, -3.0e38, ALU.add, ALU.max,
                            z_max[:, h % ZR, qt:qt + 1])
                    last.then_inc(s_z, 1)
                if (prev and h in (2, 6)) or (own and h in (10, 14)):
                    quad = b * QUADS + (h - 2) // 4 - 2
                    g = ((h - 2) // 4 + 2) % QUADS
                    turned = ot_bank[:, 0:S].rearrange("p (t j c) -> p t j c", t=QT, j=HT)
                    dve.wait_ge(s_oT, quad + 1)
                    dve.reciprocal(recip[:, :, :], turned[:, :, :, DK]).then_inc(s_rc, 1)
                    dve.wait_ge(s_rc, quad + 1)
                    if h == 10:
                        at_least(dve, s_aT_ps, b)
                    dst = attn[:, :, :].rearrange("p t (g j d) -> p t g j d", g=QUADS, j=HT)
                    dve.tensor_tensor(dst[:, :, g, :, :], turned[:, :, :, 0:DK],
                                      recip[:, :, :].unsqueeze(3).to_broadcast([P, QT, HT, DK]),
                                      ALU.mult).then_inc(s_at, 1)
                if nxt and h == 3:
                    if isinstance(b, int) and b == 0:
                        dve.wait_ge(s_rstd, 2)
                    make_normed(b + 1)
                if own and h == 4:
                    dve.wait_ge(s_v_ps, b + 1)
                    at_least(dve, s_pv, QUADS * b)
                    if isinstance(b, int) and b == 0:
                        dve.wait_ge(s_vinit, 1)
                    dve.tensor_copy(v_wide[:, :, :, 0:DK], front_bank[:, 0:QT * D].rearrange(
                        "p (t h d) -> p t h d", t=QT, h=H)).then_inc(s_v, 1)
                if nxt and h == 7:
                    make_h_t(b + 1)
                if own and h == 7:
                    dve.wait_ge(s_nrm, b + 1)
                    dve.tensor_scalar(norm_scale[:, 0, 0:HC + 1], norm[:, 0:HC + 1], NORM_EPS, None,
                                      ALU.max).then_inc(s_ns, 1)
                    dve.wait_ge(s_ns, 3 * b + 1)
                    dve.reciprocal(norm_scale[:, 1, 0:HC + 1], norm_scale[:, 0, 0:HC + 1]).then_inc(s_ns, 1)
                if own and h == 8:
                    dve.wait_ge(s_ns, 3 * b + 2)
                    at_least(dve, s_ws, 2 * b)
                    dve.tensor_tensor(norm_scale[:, 2, 0:HC], norm_scale[:, 1, 0:HC],
                                      cols[:, bass.ds(C_W1G + b * HC, HC)], ALU.mult)
                    dve.tensor_tensor(norm_scale[:, 2, HC:HC + 1], norm_scale[:, 1, HC:HC + 1],
                                      cols[:, bass.ds(C_W2G + b, 1)], ALU.mult).then_inc(s_ns, 1)
                    dve.wait_ge(s_ns, 3 * b + 3)
                    at_least(dve, s_w1T, b)
                    dve.tensor_tensor(w1_scaled[:, :, :], w1_raw[:, :, :],
                                      norm_scale[:, 2, 0:HC].unsqueeze(2).to_broadcast([P, HC, D]),
                                      ALU.mult).then_inc(s_ws, 1)
                if own and h == 9:
                    at_least(dve, s_w2T, b)
                    dve.tensor_scalar(w2_scaled[:, :], w2_raw[:, :],
                                      norm_scale[:, 2, HC:HC + 1], None, ALU.mult).then_inc(s_ws, 1)
                if prev and h == 13:
                    dve.wait_ge(s_yb, b)
                    rows = x_sb[:, bass.ds((b - 1) * QT, QT), :]
                    dve.tensor_tensor(rows, rows, tail_bank[:, 0:S].rearrange("p (t d) -> p t d", t=QT),
                                      ALU.add).then_inc(s_x2, 1)
                if nxt and h == 11:
                    split_hi(b + 1)
                if nxt and h == 12:
                    split_lo(b + 1)
                if prev and h == 0:
                    e = bass.ds(b - 1, 1)
                    dve.wait_ge(s_w1h, b)
                    dve.tensor_tensor(w1_lo[:, e, :], tail_bank[:, :].unsqueeze(1), w1_hi[:, e, :].bitcast(F32),
                                      ALU.subtract).then_inc(s_w1l, 1)
                if prev and h == 5:
                    e = bass.ds(b - 1, 1)
                    dve.wait_ge(s_w2h, b)
                    dve.tensor_tensor(w2_lo[:, e, :, :], tail_bank[:, :].rearrange("p (a k d) -> p a k d", a=1, k=HC),
                                      w2_hi[:, e, :, :].bitcast(F32), ALU.subtract).then_inc(s_w2l, 1)
                if own and not nxt:
                    if h == 1:
                        dve.wait_ge(s_x2, GB)
                        front_stats(0)
                    if h == 2:
                        front_mean_var(0)
                    if h == 6:
                        dve.wait_ge(s_sq, B * (HC + 1))
                        front_normed(0)
                    if h == 7:
                        dve.wait_ge(s_gate_ps, 1)
                        dve.tensor_copy(gate_t[:, :], front_bank[:, 0:E]).then_inc(s_gate, 1)
                    if h == 10:
                        dve.wait_ge(s_ws, 2 * B)
                        front_h2(0)
                    if h == 12:
                        front_lo(0)
                    if h in (13, 14, 15):
                        front_gates(0, h - 13)

            batches(dve, head_step)

            def split_hidden_hi(no, t):
                dve.wait_ge(s_silu, no + 1)
                at_least(dve, s_l2, no - HR + 1)
                dve.tensor_copy(h_hi[t % HR], hidden[:, t % HR, :]).then_inc(s_hhi[0], 1)

            def split_hidden_lo(g, t):
                dve.wait_ge(s_hhi[t % 2], N1 // 2 * g + t // 2 + 1)
                dve.tensor_tensor(h_lo[:, t % HR, :], hidden[:, t % HR, :], h_hi[t % HR].bitcast(F32),
                                  ALU.subtract).then_inc(s_hlo, 1)

            def expert_step(g, own, prev, nxt):
                for t in range(N1):
                    if not prev and t + CLOSING < H:
                        head_step(B, t + CLOSING, False, True, False)
                    if own and t % 2 == 0:
                        split_hidden_hi(N1 * g + t, t)
                    if own and t % 2 == 1:
                        split_hidden_lo(g, t)
                    if (own and t % HC == 3 and t > 3) or (prev and t == 3):
                        e = (t // HC - 1) % E
                        no = E * g + t // HC - 1
                        dve.wait_ge(s_l2, HC * (no + 1))
                        dve.wait_ge(s_wide, no + 1)
                        if e == 0:
                            at_least(dve, s_gated2, g)
                        elif t == 3:
                            dve.wait_ge(s_sum, (E - 1) * (g - 1) + e - 2)
                        else:
                            at_least(dve, s_sum, (E - 1) * g + max(e - 2, 0))
                        dve.scalar_tensor_tensor(out=summed if e == 0 else masked[:, e % 2, :],
                                                 in0=bank[2 + e % 2][:, :], scalar=cols[:, C_B2 + e:C_B2 + e + 1],
                                                 in1=mask_wide[:, e % 2, :], op0=ALU.add,
                                                 op1=ALU.mult).then_inc(s_masked, 1)
                    if prev and t == 10:
                        dve.wait_ge(s_back, g)
                        at = bass.ds((g - 1) * GT, GT)
                        dve.tensor_tensor(x_sb[:, at, :], x_sb[:, at, :],
                                          bank[5][:, :].rearrange("p (t d) -> p t d", t=GT), ALU.add).then_inc(s_final, 1)
                    if nxt and t == 8:
                        front_stats(g + 1)
                    if nxt and t == 9:
                        front_mean_var(g + 1)
                    if nxt and t == 14:
                        front_normed(g + 1)
                    if nxt and t == 18:
                        front_h2(g + 1)
                    if nxt and t == 22:
                        front_lo(g + 1)
                    if nxt and t in (24, 25, 26):
                        front_gates(g + 1, t - 24)
                    if own and t % 2 == 0:
                        split_hidden_lo(g, t)

            groups(dve, expert_step)

        @block.scalar
        def _(act):
            act.dma_start(gate_rows[:, :], gate_v).then_inc(s_gate_in, 16)
            act.dma_start(gate_g_col[:, :], gate_g.rearrange("(e a) -> e a", a=1)).then_inc(s_gate_in, 16)
            act.dma_start(gate_b_row[:, :], bass.AP(gate_b.tensor, 0, [[0, P], [1, E]])).then_inc(s_gate_in, 16)
            act.wait_ge(s_cols, 16)
            act.activation(silu_c[:, 0, :], cols[:, C_C:C_C + B], ACT.Exp, scale=-1.0).then_inc(s_cexp, 1)

            def evacuate_qk(b):
                act.wait_ge(s_qk_ps, b + 1)
                at_least(act, s_lo, b)
                act.activation(qk[:, 0, :], front_bank[:, 0:S], ACT.Identity, bias=bq_scaled[:, 0:1],
                               scale=SCORE_SCALE).then_inc(s_qk, 1)
                act.activation(qk[:, 1, :], front_bank[:, S:2 * S], ACT.Identity,
                               bias=cols[:, C_BK:C_BK + 1]).then_inc(s_qk, 1)

            def evacuate_stack(b, g):
                act.wait_ge(s_rep_ps, QUADS * b + g + 1)
                at_least(act, s_score, H * (b - 1) + HT * (g + 1))
                act.activation(stack[:, g, :, :], front_bank[:, :].rearrange("p (i s) -> p i s", i=2),
                               ACT.Copy).then_inc(s_rep, 1)

            act.wait_ge(s_bq, 1)
            evacuate_qk(0)
            evacuate_stack(0, 0)

            def front_mask(g):
                act.wait_ge(s_mask_ps, g + 1)
                act.activation(mask_t[:, bass.ds(g, 1), :], front_bank[0:E, :].unsqueeze(1), ACT.Copy).then_inc(s_mask, 1)

            def front_hi(g):
                act.wait_ge(s_h2, g + 1)
                act.activation(x_hi[:, bass.ds(g, 1), :], h2_t[:, :].unsqueeze(1), ACT.Copy).then_inc(s_xhi, 1)

            def head_step(b, h, own, prev, nxt):
                if own and h < QUADS - 1:
                    evacuate_stack(b, h + 1)
                if (own and h >= 3) or (prev and h < 3):
                    n = b * H + h - 3
                    slot = (h - 3) % PR
                    act.wait_ge(s_t, n + 1)
                    if slot % HT == 0:
                        at_least(act, s_pv, b * QUADS + (h - 3) // HT - 1)
                    act.activation(probs[:, slot, :, :],
                                   turned_bank[(h - 3) % 2][:, :].rearrange("p (k q) -> p k q", k=QT),
                                   ACT.Exp, scale=-1.0).then_inc(s_p, 1)
                if (prev and h == 3) or (own and h in (7, 11, 15)):
                    quad = b * QUADS + (h - 7) // 4
                    act.wait_ge(s_pv, quad + 1)
                    at_least(act, s_oT, quad)
                    act.activation(o_sb[:, :], pv_bank[:, 0:S], ACT.Copy).then_inc(s_o, 1)
                if own and h < 3:
                    if h == 0:
                        act.wait_ge(s_exp_w, 32 * (b + 1))
                        at_least(act, s_nrm, b)
                    for k in ((0, 1), (2,), (3,))[h]:
                        act.activation(squares[:, k * D:(k + 1) * D], w1_raw[:, k, :],
                                       ACT.Square, accum_out=norm_sq[:, k:k + 1]).then_inc(s_sq, 1)
                if prev and h == 3:
                    act.wait_ge(s_w2T, b)
                    act.activation(w2_hi[:, bass.ds(b - 1, 1), :, :],
                                   tail_bank[:, :].rearrange("p (a k d) -> p a k d", a=1, k=HC),
                                   ACT.Copy).then_inc(s_w2h, 1)
                if own and h == 4:
                    act.wait_ge(s_sq, (HC + 1) * b + HC)
                    act.activation(squares[:, :], w2_raw[:, :], ACT.Square,
                                   accum_out=norm_sq[:, HC:HC + 1]).then_inc(s_sq, 1)
                if prev and h == 8:
                    act.wait_ge(s_aT_ps, b)
                    act.activation(attn_t[:, :], tail_bank[:, 0:S], ACT.Identity,
                                   bias=cols[:, C_BV:C_BV + 1]).then_inc(s_aT, 1)
                if prev and h == 10:
                    act.wait_ge(s_y, b)
                    act.wait_ge(s_mod, 12)
                    row = bass.ds(b - 1, 1)
                    act.activation(gated_t[:, :], tail_bank[:, S:2 * S], ACT.Identity, bias=ga_col[:, 1, row],
                                   scale=ga_col[:, 0, row]).then_inc(s_yg, 1)
                if nxt and h == 9:
                    evacuate_qk(b + 1)
                if nxt and h == 14:
                    evacuate_stack(b + 1, 0)
                if own and h == 15:
                    act.wait_ge(s_w1T, b + 1)
                    act.activation(w1_hi[:, bass.ds(b, 1), :], tail_bank[:, :].unsqueeze(1),
                                   ACT.Copy).then_inc(s_w1h, 1)
                if own and not nxt:
                    if h == 11:
                        front_hi(0)
                if not own and h == 2:
                    front_mask(0)

            batches(act, head_step)

            def expert_step(g, own, prev, nxt):
                for t in range(N1):
                    if not prev and t + CLOSING < H:
                        head_step(B, t + CLOSING, False, True, False)
                    if own:
                        e = t // HC
                        no = N1 * g + t
                        act.wait_ge(s_l1, no + 1)
                        at_least(act, s_hlo, no - HR + 1)
                        act.activation(hidden[:, t % HR, :], bank[t % 2][:, :], ACT.Silu,
                                       bias=cols[:, C_B1 + t:C_B1 + t + 1]).then_inc(s_silu, 1)
                        if t % HC == 2:
                            act.wait_ge(s_wide_ps, E * g + e + 1)
                            at_least(act, s_masked, E * g + e - 1)
                            act.activation(mask_wide[:, e % 2, :], pv_bank[:, :], ACT.Copy).then_inc(s_wide, 1)
                        if t % 2 == 1:
                            act.wait_ge(s_silu, no + 1)
                            at_least(act, s_l2, no - HR + 1)
                            act.activation(h_hi[t % HR], hidden[:, t % HR, :], ACT.Copy).then_inc(s_hhi[1], 1)
                    if prev and t == 6:
                        act.wait_ge(s_sum, (E - 1) * g)
                        for i in range(GB):
                            last = act.activation(gated2[:, i * S:(i + 1) * S], summed[:, i * S:(i + 1) * S],
                                                  ACT.Copy, scale=gb_col[:, bass.ds((g - 1) * GB + i, 1)])
                        last.then_inc(s_gated2, 1)
                    if nxt and t == 20:
                        front_hi(g + 1)
                    if nxt and t == 30:
                        front_mask(g + 1)

            groups(act, expert_step)

        @block.tensor
        def _(pe):
            def turn(dst, src, n=P):
                return pe.transpose(dst, src, ident[0:n, 0:n])

            def turn_normed(b):
                pe.wait_ge(s_norm, b + 1)
                at_least(pe, s_v, b)
                for qt in range(QT):
                    last = turn(front_bank[:, qt * P:(qt + 1) * P], normed[:, qt, :])
                last.then_inc(s_hT_ps, 1)

            def project_qk(b):
                pe.wait_ge(s_hT, b + 1)
                for i in range(2):
                    last = pe.matmul(front_bank[:, i * S:(i + 1) * S], w_t[:, i, :], h_t[:, :], start=True, stop=True)
                last.then_inc(s_qk_ps, 1)

            def make_stack(b, g):
                pe.wait_ge(s_lo, b + 1)
                at_least(pe, s_rep, QUADS * b + g)
                for i in range(2):
                    for part, lo in ((qk_hi, 0), (qk_lo, 1)):
                        choose = sel[:, 2 * i + lo, g, :, :, :].rearrange("p j r d -> p (j r d)")
                        last = pe.matmul(front_bank[:, i * S:(i + 1) * S], choose, part[:, i, :],
                                         start=(lo == 0), stop=(lo == 1))
                last.then_inc(s_rep_ps, 1)

            pe.wait_ge(s_ident, 1)
            turn_normed(0)
            pe.wait_ge(s_wmod, 16)
            pe.wait_ge(s_sc, 3)
            for j in range(6):
                last = pe.matmul(bank[2][:, j * B:(j + 1) * B], wmod_sb[:, j * D:(j + 1) * D], silu_c[:, 0, :],
                                 start=True, stop=True)
            last.then_inc(s_mod_ps, 1)
            pe.wait_ge(s_w, 16)
            project_qk(0)
            pe.wait_ge(s_sel, 8)
            for g in range(2):
                make_stack(0, g)

            def front_turn(g):
                pe.wait_ge(s_norm2, g + 1)
                at_least(pe, s_mask, g)
                for t in range(GT):
                    last = turn(front_bank[:, t * P:(t + 1) * P], normed2[:, t, :])
                last.then_inc(s_h2_ps, 1)

            def front_logits(g):
                pe.wait_ge(s_h2, g + 1)
                pe.wait_ge(s_gate, 1)
                for t in range(GT):
                    last = pe.matmul(front_bank[:, t * E:(t + 1) * E], h2_t[:, t * P:(t + 1) * P], gate_t[:, :],
                                     start=True, stop=True)
                last.then_inc(s_logit_ps, 1)

            def front_mask(g):
                pe.wait_ge(s_chosen, 2 * g + 2)
                for t in range(GT):
                    last = turn(front_bank[0:E, t * P:(t + 1) * P], chosen[:, 2, t, :])
                last.then_inc(s_mask_ps, 1)

            def head_step(b, h, own, prev, nxt):
                n = b * H + h
                if own:
                    g, j = h // HT, h % HT
                    if j == 0:
                        pe.wait_ge(s_rep, QUADS * b + g + 1)
                    at_least(pe, s_z, n - 1)
                    for qt in range(QT):
                        part = stack[32 * j:32 * (j + 1), g, :, :]
                        last = pe.matmul(score_bank[h % 2][:, qt * S:(qt + 1) * S],
                                         part[:, 0, qt * P:(qt + 1) * P], part[:, 1, :], start=True, stop=True)
                    last.then_inc(s_score, 1)
                if (own and h >= 3) or (prev and h < 3):
                    m = b * H + h - 3
                    slot = (h - 3) % ZR
                    pe.wait_ge(s_w_sub, m + 1)
                    at_least(pe, s_p, m - 1)
                    for qt in range(QT):
                        for kt in range(QT):
                            at = kt * S + qt * P
                            last = turn(turned_bank[(h - 3) % 2][:, at:at + P],
                                        w[:, slot, qt, kt * P:(kt + 1) * P])
                    last.then_inc(s_t, 1)
                if (prev and h == 3) or (own and h in (7, 11, 15)):
                    quad = b * QUADS + (h - 7) // 4
                    g = ((h - 7) // 4) % QUADS
                    pe.wait_ge(s_p, HT * (quad + 1))
                    at_least(pe, s_o, quad)
                    if h == 7:
                        pe.wait_ge(s_v, b + 1)
                    for kt in range(QT):
                        for j in range(HT):
                            last = pe.matmul(pv_bank[32 * j:32 * (j + 1), 0:S], v_wide[:, kt, HT * g + j, :],
                                             probs[:, (HT * g + j) % PR, kt, :], start=(kt == 0),
                                             stop=(kt == QT - 1), skip_group_check=True)
                    last.then_inc(s_pv, 1)
                if (prev and h in (1, 5)) or (own and h in (9, 13)):
                    quad = b * QUADS + (h - 1) // 4 - 2
                    pe.wait_ge(s_o, quad + 1)
                    at_least(pe, s_at, quad)
                    for qt in range(QT):
                        last = turn(ot_bank[:, qt * P:(qt + 1) * P], o_sb[:, qt * P:(qt + 1) * P])
                    last.then_inc(s_oT, 1)
                if own and h < 2:
                    make_stack(b, h + 2)
                if own and h == 3:
                    pe.wait_ge(s_rep, QUADS * (b + 1))
                    for qt in range(QT):
                        last = pe.matmul(front_bank[:, qt * D:(qt + 1) * D], h_t[:, qt * P:(qt + 1) * P],
                                         w_t[:, 2, :], start=True, stop=True)
                    last.then_inc(s_v_ps, 1)
                if nxt and h == 6:
                    turn_normed(b + 1)
                if prev and h == 8:
                    pe.wait_ge(s_at, QUADS * b)
                    at_least(pe, s_w2l, b)
                    for qt in range(QT):
                        last = turn(tail_bank[:, qt * P:(qt + 1) * P], attn[:, qt, :])
                    last.then_inc(s_aT_ps, 1)
                if prev and h == 10:
                    pe.wait_ge(s_aT, b)
                    pe.matmul(tail_bank[:, S:2 * S], w_t[:, 3, :], attn_t[:, :], start=True,
                              stop=True).then_inc(s_y, 1)
                if prev and h == 12:
                    pe.wait_ge(s_yg, b)
                    for qt in range(QT):
                        last = turn(tail_bank[:, qt * P:(qt + 1) * P], gated_t[:, qt * P:(qt + 1) * P])
                    last.then_inc(s_yb, 1)
                if nxt and h == 9:
                    project_qk(b + 1)
                if own and h == 15:
                    pe.wait_ge(s_ws, 2 * b + 1)
                    at_least(pe, s_x2, b)
                    for k in range(HC):
                        last = turn(tail_bank[:, k * P:(k + 1) * P], w1_scaled[:, k, :])
                    last.then_inc(s_w1T, 1)
                if nxt and h >= H - 2:
                    make_stack(b + 1, h - (H - 2))
                if prev and h == 2:
                    pe.wait_ge(s_ws, 2 * b)
                    pe.wait_ge(s_w1l, b)
                    for k in range(HC):
                        last = turn(tail_bank[:, k * P:(k + 1) * P], w2_scaled[:, k * P:(k + 1) * P])
                    last.then_inc(s_w2T, 1)
                if own and not nxt:
                    if h == 6:
                        pe.wait_ge(s_gsq, 4)
                        pe.wait_ge(s_v, B)
                        turn(front_bank[:, 0:E], gate_scaled[:, :], E).then_inc(s_gate_ps, 1)
                    if h == 9:
                        pe.wait_ge(s_gate, 1)
                        front_turn(0)
                    if h == 12:
                        front_logits(0)
                if not own and h == 1:
                    front_mask(0)

            batches(pe, head_step)

            def first_product(g, t):
                e, k = t // HC, t % HC
                no = N1 * g + t
                if t == 0:
                    pe.wait_ge(s_xlo, g + 1)
                at_least(pe, s_silu, no - 1)
                part = slice(k * P, (k + 1) * P)
                for i, (weights, tokens) in enumerate(((w1_hi, x_hi), (w1_hi, x_lo), (w1_lo, x_hi))):
                    last = pe.matmul(bank[t % 2][:, :], weights[:, e, part], tokens[:, bass.ds(g, 1), :],
                                     start=(i == 0), stop=(i == 2))
                last.then_inc(s_l1, 1)

            def second_product(g, t):
                e, k = t // HC, t % HC
                if k == 0:
                    at_least(pe, s_masked, E * g + e - 1)
                pe.wait_ge(s_hlo, N1 * g + t + 1)
                hi, lo = h_hi[t % HR], h_lo[:, t % HR, :]
                for i, (weights, part) in enumerate(((w2_hi, hi), (w2_hi, lo), (w2_lo, hi))):
                    last = pe.matmul(bank[2 + e % 2][:, :], weights[:, e, k, :], part,
                                     start=(k == 0 and i == 0), stop=(k == HC - 1 and i == 2))
                last.then_inc(s_l2, 1)

            def expert_step(g, own, prev, nxt):
                for t in range(N1):
                    if not prev and t + CLOSING < H:
                        head_step(B, t + CLOSING, False, True, False)
                    if own:
                        first_product(g, t)
                    if own and t >= LAG:
                        second_product(g, t - LAG)
                    if prev and t < LAG:
                        second_product(g - 1, N1 + t - LAG)
                    if own and t % HC == 1:
                        e = t // HC
                        if e == 0:
                            pe.wait_ge(s_mask, g + 1)
                            pe.wait_ge(s_o, QUADS * B)
                        copied = counted(pe, E * g + e)
                        pe.wait_ge(s_choose, 1)
                        at_least(pe, s_wide, copied)
                        pe.matmul(pv_bank[:, :], choose[:, e, :], mask_t[:, bass.ds(g, 1), :], start=True,
                                  stop=True).then_inc(s_wide_ps, 1)
                    if prev and t == 8:
                        pe.wait_ge(s_gated2, g)
                        for i in range(GT):
                            last = turn(bank[5][:, i * P:(i + 1) * P], gated2[:, i * P:(i + 1) * P])
                        last.then_inc(s_back, 1)
                    if nxt and t == 16:
                        front_turn(g + 1)
                    if nxt and t == 21:
                        front_logits(g + 1)
                    if nxt and t == 29:
                        front_mask(g + 1)

            groups(pe, expert_step)


_ATTENTION = ('L0_attn_Wq', 'L0_attn_Wk', 'L0_attn_Wv', 'L0_attn_Wo')
_COLUMNS = {"c": 'L0_c', "bq": 'L0_attn_bq', "bk": 'L0_attn_bk', "bv": 'L0_attn_bv', "bo": 'L0_attn_bo',
            "b1": 'L0_ffn_b1', "w1_g": 'L0_ffn_w1_g', "w2_g": 'L0_ffn_w2_g', "b2": 'L0_ffn_b2'}


def kernel(**inputs):
    import numpy as _np
    import concourse.bacc as _bacc
    from concourse import mybir as _mybir
    from concourse.bass_utils import run_bass_kernel_spmd as _run

    nc = _bacc.Bacc("TRN2", target_bir_lowering=False, num_devices=1)
    D = inputs['L0_attn_x'].shape[2]
    rel = inputs['L0_attn_rel_bias']
    S = inputs['L0_attn_x'].shape[1]
    reach = (rel.shape[1] - 1) // 2
    at = _np.clip(_np.arange(2 * S) - (S - 1), -reach, reach) + reach
    E, HID = inputs['L0_ffn_b1'].shape
    places, _ = column_places(inputs['L0_c'].shape[0], E, HID // P)
    columns = _np.concatenate([inputs[_COLUMNS[name]].reshape(-1, D) for name in places], axis=0).T
    ins = {
        "x": inputs['L0_attn_x'],
        "w_in_out": _np.stack([inputs[name].T for name in _ATTENTION], axis=1),
        "columns": columns,
        "rel_ext": rel[:, at],
        "gate_v": inputs['L0_ffn_gate_v'], "gate_g": inputs['L0_ffn_gate_g'], "gate_b": inputs['L0_ffn_gate_b'],
        "w1_v": inputs['L0_ffn_w1_v'], "w2_v": inputs['L0_ffn_w2_v'], "wmod": inputs['L0_wmod'],
    }
    arrays, args = {}, []
    for name, a in ins.items():
        a = _np.ascontiguousarray(a)
        arrays[f"in_{name}_dram"] = a
        args.append(nc.dram_tensor(f"in_{name}_dram", a.shape, _mybir.dt.from_np(a.dtype), kind="ExternalInput").ap())
    out = nc.dram_tensor("out_0_dram", inputs['L0_attn_x'].shape, _mybir.dt.float32, kind="ExternalOutput").ap()
    adaln_block_kernel(nc, *args, out)
    r = _run(nc, [arrays], core_ids=[0])
    return r.results[0]["out_0_dram"]
```

```python
from contextlib import ExitStack

import concourse.bass as bass
from concourse import mybir

F32 = mybir.dt.float32
F32R = mybir.dt.float32r
U32 = mybir.dt.uint32
ALU = mybir.AluOpType
ACT = mybir.ActivationFunctionType
AX = mybir.AxisListType

P = 128
LN_EPS = 1e-5
NORM_EPS = 1e-12
GATE_FLOOR = 0.25
LOG_SMALLEST = -104.0


def at_least(engine, semaphore, count):
    if not isinstance(count, int) or count > 0:
        engine.wait_ge(semaphore, count)


def counted(engine, count):
    if not isinstance(count, int):
        engine.compute_val(count)
    return count


def column_places(B, E, HC):
    places, at = {}, 0
    for name, n in (("c", B), ("bq", 1), ("bk", 1), ("bv", 1), ("bo", 1), ("b1", E * HC), ("w1_g", E * HC),
                    ("w2_g", E), ("b2", E)):
        places[name] = at
        at += n
    return places, at


def adaln_block_kernel(nc, x, w_in_out, columns, rel_ext, gate_v, gate_g, gate_b, w1_v, w1_in_hid, w2_v,
                       w2_hid_out, wmod, out):
    B, S, D = x.shape
    H = rel_ext.shape[0]
    DK = D // H
    E, HID, _ = w1_v.shape
    QT = S // P
    TILES = B * QT
    HT = 4
    QUADS = H // HT
    PAIRS = QUADS // 2
    C_SUM = 2 * DK
    REP = P // (HT * DK)
    HC = HID // P
    GROUP = 512
    GT = GROUP // P
    GB = GROUP // S
    GROUPS = B * S // GROUP
    BW = S + P
    SCORE_SCALE = float(DK) ** -0.5
    assert D == P and S == 2 * P and HT * DK * REP == P and B == E and E == 8

    places, COLS = column_places(B, E, HC)
    C_C, C_BQ, C_BK, C_BV, C_BO = (places[name] for name in ("c", "bq", "bk", "bv", "bo"))
    C_B1, C_W1G, C_W2G, C_B2 = (places[name] for name in ("b1", "w1_g", "w2_g", "b2"))

    with ExitStack() as ctx:
        def sb(name, shape, dt=F32):
            return ctx.enter_context(nc.sbuf_tensor(name, shape, dt))

        def sem(name):
            return ctx.enter_context(nc.semaphore(name))

        bank = [ctx.enter_context(nc.psum_tensor(f"bank{i}", [P, 512], F32)) for i in range(8)]
        score_bank, turned_bank = bank[0:2], bank[2:4]
        pv_bank, ot_bank, front_bank, tail_bank = bank[4:8]
        stack_bank = (front_bank, tail_bank)

        ident = sb("ident", [P, P])
        sel = sb("sel", [P, 2, QUADS, HT, REP, DK], F32R)
        w_t = sb("w_t", [P, 4, D])
        cols = sb("cols", [P, COLS])
        bq_scaled = sb("bq_scaled", [P, 1])
        silu_c = sb("silu_c", [P, 3, B])
        wmod_sb = sb("wmod_sb", [P, 6 * D])
        mod = sb("mod", [P, 6, B])
        gate_tmp = sb("gate_tmp", [P, 2, 2, B])
        ga_col = sb("ga_col", [P, 2, B])
        gb_col = sb("gb_col", [P, B])
        band = sb("band", [P, H, BW])

        x_sb = sb("x_sb", [P, TILES, D])
        stats = sb("stats", [P, QT, 6])
        mean_var = sb("mean_var", [P, QT, 2])
        rstd = sb("rstd", [P, QT])
        minus_half = sb("minus_half", [P, GT])
        half = sb("half", [P, 8])

        normed = sb("normed", [P, QT, D])
        h_t = sb("h_t", [P, S])
        qk = sb("qk", [P, 2, S])
        qk_parts = sb("qk_parts", [P, 2, 2, S], F32R)
        stack = sb("stack", [P, QUADS, 2, S], F32R)
        v_wide = sb("v_wide", [P, QT, H, 32])
        v_pairs = v_wide[:, :, :, :].rearrange("p t (m u j) c -> p (t m) u j c", m=PAIRS, u=2)
        ZR = 4
        z = sb("z", [P, ZR, QT, S])
        z_max = sb("z_max", [P, ZR, QT])
        w = sb("w", [P, ZR, QT, S])
        PR = 8
        probs = sb("probs", [P, PR, QT, S])
        o_sb = sb("o_sb", [P, S])
        recip = sb("recip", [P, QT, HT, 2])
        attn = sb("attn", [P, QT, D])
        attn_t = sb("attn_t", [P, S])
        gated_t = sb("gated_t", [P, S])

        w1_raw = sb("w1_raw", [P, HC, D])
        w2_raw = sb("w2_raw", [P, HID])
        squares = sb("squares", [P, HID])
        norm_sq = sb("norm_sq", [P, 8])
        norm = sb("norm", [P, 8])
        norm_scale = sb("norm_scale", [P, 2, 8])
        w1_t = sb("w1_t", [P, HID])
        w2_t = sb("w2_t", [P, HC, D])
        w_scale = sb("w_scale", [P, E, HC + 1])
        w1_hi = sb("w1_hi", [P, E, HID], F32R)
        w1_lo = sb("w1_lo", [P, E, HID], F32R)
        w2_hi = sb("w2_hi", [P, E, HC, D], F32R)
        w2_lo = sb("w2_lo", [P, E, HC, D], F32R)

        gate_rows = sb("gate_rows", [E, D])
        gate_g_col = sb("gate_g_col", [E, 1])
        gate_b_row = sb("gate_b_row", [P, E])
        gate_sq = sb("gate_sq", [E, D])
        gate_norm = sb("gate_norm", [E, 4])
        gate_scaled = sb("gate_scaled", [E, D])
        gate_t = sb("gate_t", [P, E])
        stats2 = sb("stats2", [P, GT, 6])
        mean_var2 = sb("mean_var2", [P, GT, 2])
        rstd2 = sb("rstd2", [P, GT])
        expert_no = sb("expert_no", [P, GT, E])
        logits = sb("logits", [P, 3, GT, E])
        top = sb("top", [P, GT])
        top8 = sb("top8", [P, GT, 8])
        top_at = sb("top_at", [P, GT, 8], U32)
        top_no = sb("top_no", [P, GT, 2])
        chosen = sb("chosen", [P, 3, GT, E])
        mask_t = sb("mask_t", [E, GROUP])
        mask_rows = nc.dram_tensor("mask_rows", [E, GROUP], F32, kind="Internal").ap()
        mask_wide = probs[:, :, :, :].rearrange("p e k s -> p e (k s)")
        x_hi = stack[:, :, :, :].rearrange("p g i s -> p g (i s)")
        x_lo = sb("x_lo", [P, GROUPS, GROUP], F32R)
        HR = 4
        hidden = z[:, :, :, :].rearrange("p i t s -> p i (t s)")
        h_lo = sb("h_lo", [P, HR, GROUP], F32R)
        h_hi_rest = sb("h_hi_rest", [P, HR - 2, GROUP], F32R)
        h_hi = [qk_parts[:, i, :, :].rearrange("p i s -> p (i s)") for i in range(2)] + [
            h_hi_rest[:, i, :] for i in range(HR - 2)]
        normed2 = sb("normed2", [P, GT, D])
        h2_t = w1_raw[:, :, :].rearrange("p k d -> p (k d)")
        spare = band[:, :, :].rearrange("p h u -> p (h u)").rearrange("p (i n) -> p i n", n=GROUP)
        silu_first = sb("silu_first", [P, 1])
        y_out, masked = spare[:, 0:2, :], spare[:, 2:4, :]
        summed, gated2 = spare[:, 4, :], spare[:, 5, :]

        s_x = [sem(f"x_loaded{i}") for i in range(2)]
        s_cols = sem("columns_loaded")
        s_bq = sem("bq_scaled_done")
        s_w = sem("weights_loaded")
        s_wmod = sem("wmod_loaded")
        s_band = [sem(f"band_loaded{i}") for i in range(QUADS)]
        s_exp_w = sem("expert_weights_loaded")
        s_ident0 = sem("ident_zeroed")
        s_ident = sem("ident_ready")
        s_consts = sem("pool_constants_ready")
        s_sel = sem("sel_ready")
        s_vz = sem("v_wide_zeroed")
        s_vinit = sem("v_wide_ready")
        s_cexp = sem("c_exp_done")
        s_sc = sem("silu_c_step")
        s_mod_ps = sem("mod_in_psum")
        s_mod = sem("mod_step")
        s_warm = sem("warm_up_done")
        s_stats = sem("stats_done")
        s_mv = sem("mean_var_done")
        s_eps = sem("eps_added")
        s_rstd = sem("rstd_done")

        s_norm = sem("normed_ready")
        s_hT_ps = sem("h_t_in_psum")
        s_hT = sem("h_t_ready")
        s_qk_ps = sem("qk_in_psum")
        s_qk = sem("qk_ready")
        s_hi = sem("qk_hi_ready")
        s_lo = sem("qk_lo_ready")
        s_rep_ps = sem("stack_in_psum")
        s_rep = sem("first_stacks_ready")
        s_rep_last = sem("last_stack_ready")
        s_v_ps = sem("v_in_psum")
        s_v = sem("v_ready")
        s_score = sem("score_done")
        s_z = sem("z_ready")
        s_w_sub = sem("w_ready")
        s_t = sem("w_turned")
        s_p = sem("probs_ready")
        s_pv = sem("pv_done")
        s_o = sem("o_evacuated")
        s_oT = sem("o_turned")
        s_rc = sem("recip_done")
        s_at = sem("attn_ready")
        s_aT_ps = sem("attn_turned")
        s_aT = sem("attn_t_ready")
        s_y = sem("y_done")
        s_yg = sem("gated_t_ready")
        s_yb = sem("gated_turned")
        s_x2 = sem("x2_ready")

        s_sq = sem("squares_done")
        s_nrm = sem("norm_done")
        s_ns = sem("norm_scale_step")
        s_exp_t = sem("expert_weights_turned_loaded")
        s_w1h = sem("w1_hi_done")
        s_w2h = sem("w2_hi_done")
        s_w1l = sem("w1_lo_done")
        s_w2l = sem("w2_lo_done")
        s_out = sem("out_stored")

        s_gate_in = sem("gate_inputs_loaded")
        s_gsq = sem("gate_prep_step")
        s_gnorm = sem("gate_norm_done")
        s_gate_ps = sem("gate_t_in_psum")
        s_gate = sem("gate_t_ready")
        s_no = sem("expert_numbers_ready")
        s_stats2 = sem("stats2_done")
        s_eps2 = sem("eps2_step")
        s_rstd2 = sem("rstd2_done")
        s_norm2 = sem("normed2_ready")
        s_h2_ps = sem("h2_in_psum")
        s_h2 = sem("h2_ready")
        s_xhi = sem("x_hi_ready")
        s_xlo = sem("x_lo_ready")
        s_logit_ps = sem("logits_in_psum")
        s_logit = sem("logits_step")
        s_top = sem("top_step")
        s_chosen = sem("chosen_step")
        s_mask_ps = sem("mask_t_in_psum")
        s_mask = sem("mask_t_ready")
        s_mask_out = sem("mask_in_dram")
        s_wide = [sem(f"mask_wide_loaded{i}") for i in range(2)]
        s_l1 = sem("hidden_in_psum")
        s_silu = sem("hidden_ready")
        s_hhi = [sem(f"h_hi_ready_{by}") for by in ("dve", "act")]
        s_hlo = sem("h_lo_ready")
        s_l2 = sem("l2_done")
        s_yout = sem("expert_output_ready")
        s_masked = sem("masked_ready")
        s_sum = sem("summed_step")
        s_gated2 = sem("gated2_ready")
        s_back = sem("gated2_turned")
        s_final = sem("final_ready")

        block = ctx.enter_context(nc.Block())
        x_dram = x.rearrange("b (t p) d -> p (b t) d", p=P)
        w1_dram = w1_v.rearrange("e (k p) d -> p (e k) d", p=P)
        w2_dram = w2_v.rearrange("e d h -> d e h")
        w1_t_dram = w1_in_hid.rearrange("e d h -> d e h")
        w2_t_dram = w2_hid_out.rearrange("e (k p) d -> p (e k) d", p=P)
        out_dram = out.rearrange("b (t p) d -> p (b t) d", p=P)

        def band_dram(g):
            width = rel_ext.shape[1]
            return bass.AP(rel_ext.tensor, HT * g * width, [[1, P], [width, HT], [1, BW]])

        CLOSING = 3

        def batches(engine, head_step):
            for h in range(H):
                head_step(0, h, True, False, True)
            with engine.Fori(1, B - 1) as b:
                for h in range(H):
                    head_step(b, h, True, True, True)
            for h in range(H):
                head_step(B - 1, h, True, True, False)
            for h in range(CLOSING):
                head_step(B, h, False, True, False)

        N1 = E * HC
        HALF_E = E // 2
        LAG = 3

        def parts(whole):
            n = GROUP if whole else GROUP // 2
            return [(i, slice(i * n, (i + 1) * n)) for i in range(GROUP // n)]

        def groups(engine, step):
            step(0, True, False, True)
            with engine.Fori(1, GROUPS - 1) as g:
                step(g, True, True, True)
            step(GROUPS - 1, True, True, False)
            step(GROUPS, False, True, False)

        @block.sync
        def _(sp):
            sp.dma_start(x_sb[:, 0:QT, :], x_dram[:, 0:QT, :]).then_inc(s_x[0], 16)
            sp.dma_start(cols[:, :], columns).then_inc(s_cols, 16)
            sp.dma_start(wmod_sb[:, :], wmod).then_inc(s_wmod, 16)
            sp.dma_start(w_t[:, :, :], w_in_out).then_inc(s_w, 16)
            sp.dma_start(x_sb[:, QT:TILES, :], x_dram[:, QT:TILES, :]).then_inc(s_x[1], 16)

            def load_band(g):
                sp.dma_start(band[:, HT * g:HT * (g + 1), :], band_dram(g)).then_inc(s_band[g], 16)

            def load_expert(e):
                sp.dma_start(w1_raw[:, :, :], w1_dram[:, bass.ds(e * HC, HC), :]).then_inc(s_exp_w, 16)
                sp.dma_start(w2_raw[:, :], w2_dram[:, bass.ds(e, 1), :]).then_inc(s_exp_w, 16)

            def load_expert_t(e):
                sp.dma_start(w1_t[:, :].unsqueeze(1), w1_t_dram[:, bass.ds(e, 1), :]).then_inc(s_exp_t, 16)
                sp.dma_start(w2_t[:, :, :], w2_t_dram[:, bass.ds(e * HC, HC), :]).then_inc(s_exp_t, 16)

            load_band(0)
            load_expert(0)
            sp.dma_start(gate_rows[:, :], gate_v).then_inc(s_gate_in, 16)
            sp.dma_start(gate_g_col[:, :], gate_g.rearrange("(e a) -> e a", a=1)).then_inc(s_gate_in, 16)
            sp.dma_start(gate_b_row[:, :], bass.AP(gate_b.tensor, 0, [[0, P], [1, E]])).then_inc(s_gate_in, 16)
            for g in range(1, QUADS):
                load_band(g)
            load_expert_t(0)
            with sp.Fori(1, E) as e:
                sp.wait_ge(s_sq, (HC + 1) * e)
                load_expert(e)
                sp.wait_ge(s_w1l, e)
                sp.wait_ge(s_w2l, e)
                load_expert_t(e)

            def spread_masks(g):
                first = isinstance(g, int) and g == 0
                ready, read, stored = counted(sp, g + 1), counted(sp, 16 * g), counted(sp, 16 * (g + 1))
                used = [counted(sp, E * (g - 1) + HALF_E * (i + 1)) for i in range(2)]
                sp.wait_ge(s_mask, ready)
                for i in range(2):
                    at_least(sp, s_wide[i], read)
                sp.dma_start(mask_rows, mask_t[:, :]).then_inc(s_mask_out, 16)
                sp.wait_ge(s_mask_out, stored)
                for i in range(2):
                    if first:
                        sp.wait_ge(s_pv, QUADS * B - 1 + i)
                    else:
                        sp.wait_ge(s_masked, used[i])
                    sp.dma_start(mask_wide[:, HALF_E * i:HALF_E * (i + 1), :], bass.AP(
                        mask_rows.tensor, HALF_E * i * GROUP, [[0, P], [GROUP, HALF_E], [1, GROUP]])).then_inc(s_wide[i], 16)

            spread_masks(0)
            with sp.Fori(1, GROUPS) as g:
                spread_masks(g)
                sp.wait_ge(s_final, g)
                sp.dma_start(out_dram[:, bass.ds((g - 1) * GT, GT), :],
                             x_sb[:, bass.ds((g - 1) * GT, GT), :]).then_inc(s_out, 16)
            for i in range(2):
                sp.wait_ge(s_final, GROUPS + i)
                at = slice((GROUPS - 1) * GT + i * QT, (GROUPS - 1) * GT + (i + 1) * QT)
                sp.dma_start(out_dram[:, at, :], x_sb[:, at, :]).then_inc(s_out, 16)
            sp.wait_ge(s_out, 16 * (GROUPS + 1))

        @block.gpsimd
        def _(pool):
            pool.memset(ident[:, :], 0.0).then_inc(s_ident0, 1)
            pool.memset(minus_half[:, :], -0.5).then_inc(s_consts, 1)
            pool.memset(half[:, :], 0.5).then_inc(s_consts, 1)
            pool.wait_ge(s_ident0, 1)
            pool.affine_select(out=ident[:, :], in_=ident[:, :], compare_op=ALU.not_equal, fill=1.0, base=0,
                               pattern=[[-1, P]], channel_multiplier=1).then_inc(s_ident, 1)
            pool.wait_ge(s_consts, 2)

            def row_rstd(b):
                pool.wait_ge(s_eps, b + 1)
                pool.tensor_tensor(rstd[:, :], mean_var[:, :, 1], minus_half[:, 0:QT], ALU.pow).then_inc(s_rstd, 1)

            pool.wait_ge(s_ident, 1)
            ones = ident[:, :].rearrange("p (g j d) -> p g j d", g=QUADS, j=HT)
            for i, (high, low) in enumerate((((0, 1), (2, 3)), ((0, 2), (1, 3)))):
                for r in high:
                    pool.tensor_copy(sel[:, i, :, :, r, :], ones).then_inc(s_sel, 1)
                for r in low:
                    for half_g in range(2):
                        to, from_ = slice(2 * half_g, 2 * half_g + 2), slice(2 - 2 * half_g, 4 - 2 * half_g)
                        pool.tensor_copy(sel[:, i, to, :, r, :], ones[:, from_, :, :]).then_inc(s_sel, 1)
                if i == 0:
                    row_rstd(0)
            pool.memset(v_wide[:, :, :, :], 0.0).then_inc(s_vz, 1)
            pool.wait_ge(s_vz, 1)
            for u in range(2):
                pool.memset(v_pairs[:, :, u, :, C_SUM + u:C_SUM + u + 1], 1.0).then_inc(s_vinit, 1)
            pool.iota(expert_no[:, :, :], pattern=[[0, GT], [1, E]], base=0, channel_multiplier=0,
                      allow_small_or_imprecise_dtypes=True).then_inc(s_no, 1)

            def front(g):
                pool.wait_ge(s_eps2, 2 * g + 2)
                pool.tensor_tensor(rstd2[:, :], mean_var2[:, :, 1], minus_half[:, 0:GT], ALU.pow).then_inc(s_rstd2, 1)

            def head_step(b, h, own, prev, nxt):
                if not own:
                    return
                n = b * H + h
                ready, turned = counted(pool, n + 1), counted(pool, n - ZR + 1)
                pool.wait_ge(s_consts, 2)
                pool.wait_ge(s_z, ready)
                at_least(pool, s_t, turned)
                for qt in range(QT):
                    sub = pool.tensor_scalar(w[:, h % ZR, qt, :], z[:, h % ZR, qt, :], -1.0,
                                             z_max[:, h % ZR, qt:qt + 1], ALU.mult, ALU.add)
                sub.then_inc(s_w_sub, 1)
                if nxt and h == 1:
                    row_rstd(b + 1)
                if not prev and h == 3:
                    pool.wait_ge(s_gsq, 1)
                    pool.tensor_tensor(gate_norm[:, 1:2], gate_norm[:, 0:1], half[0:E, 0:1],
                                       ALU.pow).then_inc(s_gnorm, 1)
                if h == 8:
                    pool.wait_ge(s_sq, (b + 1) * (HC + 1))
                    at_least(pool, s_ns, 3 * b)
                    pool.tensor_tensor(norm[:, 0:HC + 1], norm_sq[:, 0:HC + 1], half[:, 0:HC + 1],
                                       ALU.pow).then_inc(s_nrm, 1)
                if not nxt and h == 4:
                    front(0)

            batches(pool, head_step)

            def expert_step(g, own, prev, nxt):
                if prev:
                    e = E - 1
                    done = (E - 1) * (g - 1)
                    pool.wait_ge(s_sum, done + e - 1)
                    for i, part in parts(own):
                        pool.wait_ge(s_masked, E * g + i)
                        pool.tensor_tensor(summed[:, part], summed[:, part], masked[:, e % 2, part],
                                           ALU.add).then_inc(s_sum, 1)
                if not own:
                    return
                if nxt:
                    front(g + 1)
                for e in range(1, E - 1):
                    done = (E - 1) * g
                    pool.wait_ge(s_masked, E * g + e + 1)
                    at_least(pool, s_sum, done + e - 1)
                    pool.tensor_tensor(summed, summed, masked[:, e % 2, :], ALU.add).then_inc(s_sum, 1)

            groups(pool, expert_step)

        @block.vector
        def _(dve):
            def row_stats(b):
                for qt in range(QT):
                    last = dve.bn_stats(stats[:, qt, :], x_sb[:, bass.ds(b * QT + qt, 1), :])
                last.then_inc(s_stats, 1)

            def row_mean_var(b):
                seen, used = counted(dve, b + 1), counted(dve, b)
                dve.wait_ge(s_x[0], 16)
                dve.wait_ge(s_stats, seen)
                at_least(dve, s_norm, used)
                for qt in range(QT):
                    last = dve.bn_aggr(mean_var[:, qt, :], stats[:, qt, :])
                last.then_inc(s_mv, 1)
                dve.wait_ge(s_mv, b + 1)
                dve.tensor_scalar(mean_var[:, :, 1], mean_var[:, :, 1], LN_EPS, None, ALU.add).then_inc(s_eps, 1)

            def make_normed(b):
                at_least(dve, s_hT_ps, b)
                dve.wait_ge(s_rstd, b + 1)
                for qt in range(QT):
                    last = dve.tensor_scalar(normed[:, qt, :], x_sb[:, bass.ds(b * QT + qt, 1), :],
                                             mean_var[:, qt, 0:1], rstd[:, qt:qt + 1], ALU.subtract, ALU.mult)
                last.then_inc(s_norm, 1)

            def make_h_t(b):
                dve.wait_ge(s_hT_ps, b + 1)
                at_least(dve, s_v_ps, b)
                dve.tensor_scalar(h_t[:, :], front_bank[:, 0:S], mod[:, 1, bass.ds(b, 1)],
                                  mod[:, 0, bass.ds(b, 1)], ALU.mult, ALU.add).then_inc(s_hT, 1)

            def split_lo(b, i):
                own, other = (slice(0, P // 2), slice(P // 2, P))[::1 - 2 * i]
                dve.wait_ge(s_hi, 2 * b + i + 1)
                dve.tensor_tensor(qk_parts[other, i, :, :], qk[own, :, :], qk_parts[own, i, :, :].bitcast(F32),
                                  ALU.subtract).then_inc(s_lo, 1)

            dve.wait_ge(s_x[0], 16)
            row_stats(0)
            row_mean_var(0)
            dve.wait_ge(s_cols, 16)
            dve.tensor_scalar(bq_scaled[:, :], cols[:, C_BQ:C_BQ + 1], SCORE_SCALE, None, ALU.mult).then_inc(s_bq, 1)
            dve.wait_ge(s_cexp, 1)
            dve.tensor_scalar(silu_c[:, 1, :], silu_c[:, 0, :], 1.0, None, ALU.add).then_inc(s_sc, 1)
            dve.wait_ge(s_sc, 1)
            dve.reciprocal(silu_c[:, 2, :], silu_c[:, 1, :]).then_inc(s_sc, 1)
            dve.wait_ge(s_sc, 2)
            dve.tensor_tensor(silu_c[:, 0, :], silu_c[:, 2, :], cols[:, C_C:C_C + B], ALU.mult).then_inc(s_sc, 1)
            make_normed(0)
            dve.wait_ge(s_mod_ps, 1)
            dve.tensor_copy(mod[:, 0, :], bank[2][:, 0:B])
            dve.tensor_scalar(mod[:, 1, :], bank[2][:, B:2 * B], 1.0, None, ALU.add).then_inc(s_mod, 1)
            dve.wait_ge(s_mod, 1)
            make_h_t(0)
            dve.wait_ge(s_mod_ps, 2)
            dve.tensor_copy(mod[:, 2:6, :], bank[3][:, 0:4 * B].rearrange("p (j b) -> p j b", j=4)).then_inc(s_mod, 1)
            dve.wait_ge(s_mod, 2)
            dve.tensor_scalar(mod[:, 4, :], mod[:, 4, :], 1.0, None, ALU.add).then_inc(s_mod, 1)
            for i, j in enumerate((2, 5)):
                g = mod[:, j, :]
                dve.tensor_scalar(gate_tmp[:, i, 0, :], g, 0.0, 2.0, ALU.is_ge, ALU.mult).then_inc(s_mod, 1)
                dve.scalar_tensor_tensor(out=gate_tmp[:, i, 1, :], in0=g, scalar=-1.0, in1=g, op0=ALU.mult,
                                         op1=ALU.max).then_inc(s_mod, 1)
            dve.wait_ge(s_mod, 7)
            for i in range(2):
                dve.tensor_scalar(gate_tmp[:, i, 1, :], gate_tmp[:, i, 1, :], GATE_FLOOR, None,
                                  ALU.max).then_inc(s_mod, 1)
            dve.wait_ge(s_mod, 9)
            for i, o in enumerate((ga_col[:, 0, :], gb_col[:, :])):
                dve.scalar_tensor_tensor(out=o, in0=gate_tmp[:, i, 0, :], scalar=-1.0, in1=gate_tmp[:, i, 1, :],
                                         op0=ALU.add, op1=ALU.mult).then_inc(s_mod, 1)
            dve.wait_ge(s_mod, 11)
            dve.tensor_scalar(ga_col[:, 1, :], ga_col[:, 0, :], cols[:, C_BO:C_BO + 1], None,
                              ALU.mult).then_inc(s_mod, 1)
            for i in range(2):
                split_lo(0, i)

            def front_stats(g):
                for t in range(GT):
                    last = dve.bn_stats(stats2[:, t, :], x_sb[:, bass.ds(g * GT + t, 1), :])
                last.then_inc(s_stats2, 1)

            def front_mean_var(g):
                seen = counted(dve, g + 1)
                dve.wait_ge(s_no, 1)
                dve.wait_ge(s_stats2, seen)
                for t in range(GT):
                    last = dve.bn_aggr(mean_var2[:, t, :], stats2[:, t, :])
                last.then_inc(s_eps2, 1)
                dve.wait_ge(s_eps2, 2 * g + 1)
                dve.tensor_scalar(mean_var2[:, :, 1], mean_var2[:, :, 1], LN_EPS, None, ALU.add).then_inc(s_eps2, 1)

            def front_normed(g):
                dve.wait_ge(s_rstd2, g + 1)
                at_least(dve, s_h2_ps, g)
                for t in range(GT):
                    last = dve.tensor_scalar(normed2[:, t, :], x_sb[:, bass.ds(g * GT + t, 1), :],
                                             mean_var2[:, t, 0:1], rstd2[:, t:t + 1], ALU.subtract, ALU.mult)
                last.then_inc(s_norm2, 1)

            def front_h2(g):
                dve.wait_ge(s_h2_ps, g + 1)
                at_least(dve, s_logit_ps, g)
                for i in range(GB):
                    b = bass.ds(g * GB + i, 1)
                    last = dve.tensor_scalar(h2_t[:, i * S:(i + 1) * S], front_bank[:, i * S:(i + 1) * S], mod[:, 4, b],
                                             mod[:, 3, b], ALU.mult, ALU.add)
                last.then_inc(s_h2, 1)

            def front_lo(g):
                dve.wait_ge(s_xhi, g + 1)
                dve.tensor_tensor(x_lo[:, bass.ds(g, 1), :], h2_t[:, :].unsqueeze(1),
                                  x_hi[:, bass.ds(g, 1), :].bitcast(F32), ALU.subtract).then_inc(s_xlo, 1)

            def front_gates(g, part):
                wide = [P, GT, E]
                if part == 0:
                    dve.wait_ge(s_logit_ps, g + 1)
                    dve.tensor_tensor(logits[:, 0, :, :], front_bank[:, 0:GT * E].rearrange("p (t e) -> p t e", t=GT),
                                      gate_b_row[:, :].unsqueeze(1).to_broadcast(wide), ALU.add).then_inc(s_logit, 1)
                    dve.wait_ge(s_logit, 4 * g + 1)
                    dve.tensor_reduce(top[:, :], logits[:, 0, :, :], AX.X, ALU.max).then_inc(s_logit, 1)
                    dve.wait_ge(s_logit, 4 * g + 2)
                    dve.tensor_tensor(logits[:, 1, :, :], logits[:, 0, :, :],
                                      top[:, :].unsqueeze(2).to_broadcast(wide), ALU.subtract).then_inc(s_logit, 1)
                    dve.wait_ge(s_logit, 4 * g + 3)
                    dve.tensor_scalar(logits[:, 2, :, :], logits[:, 1, :, :], LOG_SMALLEST, None,
                                      ALU.max).then_inc(s_logit, 1)
                if part == 1:
                    seen = counted(dve, 4 * g + 4)
                    dve.wait_ge(s_no, 1)
                    dve.wait_ge(s_logit, seen)
                    for t in range(GT):
                        last = dve.max(top8[:, t, :], logits[:, 2, t, :])
                    last.then_inc(s_top, 1)
                    seen = counted(dve, 3 * g + 1)
                    dve.wait_ge(s_no, 1)
                    dve.wait_ge(s_top, seen)
                    for t in range(GT):
                        last = dve.max_index(top_at[:, t, :], top8[:, t, :], logits[:, 2, t, :])
                    last.then_inc(s_top, 1)
                    dve.wait_ge(s_top, 3 * g + 2)
                    dve.tensor_copy(top_no[:, :, :], top_at[:, :, 0:2]).then_inc(s_top, 1)
                if part == 2:
                    dve.wait_ge(s_top, 3 * g + 3)
                    at_least(dve, s_mask_ps, g)
                    for k in range(2):
                        last = dve.tensor_tensor(chosen[:, k, :, :], expert_no[:, :, :],
                                                 top_no[:, :, k].unsqueeze(2).to_broadcast(wide), ALU.is_equal)
                    last.then_inc(s_chosen, 1)
                    dve.wait_ge(s_chosen, 2 * g + 1)
                    dve.tensor_tensor(chosen[:, 2, :, :], chosen[:, 0, :, :], chosen[:, 1, :, :],
                                      ALU.add).then_inc(s_chosen, 1)

            def head_step(b, h, own, prev, nxt):
                n = b * H + h
                if own:
                    scored, subtracted = counted(dve, n + 1), counted(dve, n - ZR + 1)
                    dve.wait_ge(s_band[h // HT], 16)
                    dve.wait_ge(s_score, scored)
                    at_least(dve, s_w_sub, subtracted)
                    for qt in range(QT):
                        last_key = qt * P
                        last = dve.tensor_tensor_reduce(
                            z[:, h % ZR, qt, :], score_bank[h % 2][:, qt * S:(qt + 1) * S],
                            band[:, h, last_key:last_key + S][:, ::-1], 1.0, -3.0e38, ALU.add, ALU.max,
                            z_max[:, h % ZR, qt:qt + 1])
                    last.then_inc(s_z, 1)
                if (prev and h == 6) or (own and h == 14):
                    pair = b * PAIRS + (h - 6) // 8 - 1
                    m = PAIRS - 1 if h == 6 else 0
                    turned = ot_bank[:, 0:S].rearrange("p (t j c) -> p t j c", t=QT, j=HT)
                    dve.wait_ge(s_oT, pair + 1)
                    dve.reciprocal(recip[:, :, :, :], turned[:, :, :, C_SUM:C_SUM + 2]).then_inc(s_rc, 1)
                    dve.wait_ge(s_rc, pair + 1)
                    if h == 14:
                        at_least(dve, s_aT_ps, b)
                    dst = attn[:, :, :].rearrange("p t (m u j d) -> p t m u j d", m=PAIRS, u=2, j=HT)
                    for u in range(2):
                        last = dve.tensor_tensor(dst[:, :, m, u, :, :], turned[:, :, :, u * DK:(u + 1) * DK],
                                                 recip[:, :, :, u].unsqueeze(3).to_broadcast([P, QT, HT, DK]),
                                                 ALU.mult)
                    last.then_inc(s_at, 1)
                if nxt and h == 0:
                    if not prev:
                        dve.wait_ge(s_x[1], 16)
                    row_stats(b + 1)
                if nxt and h == 1:
                    row_mean_var(b + 1)
                if not prev and h == 2:
                    dve.wait_ge(s_gate_in, 48)
                    dve.tensor_tensor_reduce(gate_sq[:, :], gate_rows[:, :], gate_rows[:, :], 1.0, 0.0, ALU.mult, ALU.add,
                                             gate_norm[:, 0:1]).then_inc(s_gsq, 1)
                if not prev and h == 6:
                    dve.wait_ge(s_gnorm, 1)
                    dve.tensor_scalar(gate_norm[:, 2:3], gate_norm[:, 1:2], NORM_EPS, None, ALU.max).then_inc(s_gsq, 1)
                    dve.wait_ge(s_gsq, 2)
                    dve.reciprocal(gate_norm[:, 3:4], gate_norm[:, 2:3]).then_inc(s_gsq, 1)
                    dve.wait_ge(s_gsq, 3)
                    dve.tensor_scalar(gate_scaled[:, :], gate_rows[:, :], gate_norm[:, 3:4], gate_g_col[:, 0:1],
                                      ALU.mult, ALU.mult).then_inc(s_gsq, 1)
                if own and h == 2:
                    dve.wait_ge(s_rep_ps, QUADS * (b + 1))
                    at_least(dve, s_score, H * b)
                    dve.tensor_copy(stack[:, QUADS - 1, :, :], stack_bank[(QUADS - 1) % 2][:, :].rearrange(
                        "p (i s) -> p i s", i=2)).then_inc(s_rep_last, 1)
                if nxt and h == 3:
                    make_normed(b + 1)
                if own and h == 4:
                    dve.wait_ge(s_v_ps, b + 1)
                    at_least(dve, s_pv, QUADS * b)
                    if isinstance(b, int) and b == 0:
                        dve.wait_ge(s_vinit, 2)
                    values = front_bank[:, 0:QT * D].rearrange("p (t u j d) -> p t u j d", t=QT * PAIRS, u=2, j=HT)
                    for u in range(2):
                        last = dve.tensor_copy(v_pairs[:, :, u, :, u * DK:(u + 1) * DK], values[:, :, u, :, :])
                    last.then_inc(s_v, 1)
                if nxt and h == 7:
                    make_h_t(b + 1)
                if own and h == 11:
                    dve.wait_ge(s_nrm, b + 1)
                    dve.tensor_scalar(norm_scale[:, 0, 0:HC + 1], norm[:, 0:HC + 1], NORM_EPS, None,
                                      ALU.max).then_inc(s_ns, 1)
                    dve.wait_ge(s_ns, 3 * b + 1)
                    dve.reciprocal(norm_scale[:, 1, 0:HC + 1], norm_scale[:, 0, 0:HC + 1]).then_inc(s_ns, 1)
                if own and h == 13:
                    dve.wait_ge(s_ns, 3 * b + 2)
                    e = bass.ds(b, 1)
                    dve.tensor_tensor(w_scale[:, e, 0:HC], norm_scale[:, 1, 0:HC].unsqueeze(1),
                                      cols[:, bass.ds(C_W1G + b * HC, HC)].unsqueeze(1), ALU.mult)
                    dve.tensor_tensor(w_scale[:, e, HC:HC + 1], norm_scale[:, 1, HC:HC + 1].unsqueeze(1),
                                      cols[:, bass.ds(C_W2G + b, 1)].unsqueeze(1), ALU.mult).then_inc(s_ns, 1)
                if own and h == 9:
                    e = bass.ds(b, 1)
                    dve.wait_ge(s_w1h, b + 1)
                    dve.tensor_tensor(w1_lo[:, e, :], w1_t[:, :].unsqueeze(1), w1_hi[:, e, :].bitcast(F32),
                                      ALU.subtract).then_inc(s_w1l, 1)
                if own and h == 15:
                    e = bass.ds(b, 1)
                    dve.wait_ge(s_w2h, b + 1)
                    dve.tensor_tensor(w2_lo[:, e, :, :], w2_t[:, :, :].unsqueeze(1),
                                      w2_hi[:, e, :, :].bitcast(F32), ALU.subtract).then_inc(s_w2l, 1)
                if prev and h == 13:
                    dve.wait_ge(s_yb, b)
                    rows = x_sb[:, bass.ds((b - 1) * QT, QT), :]
                    dve.tensor_tensor(rows, rows, tail_bank[:, 0:S].rearrange("p (t d) -> p t d", t=QT),
                                      ALU.add).then_inc(s_x2, 1)
                if nxt and h in (11, 12):
                    split_lo(b + 1, h - 11)
                if own and not nxt:
                    if h == 1:
                        dve.wait_ge(s_x2, GB)
                        front_stats(0)
                    if h == 2:
                        front_mean_var(0)
                    if h == 6:
                        front_normed(0)
                    if h == 7:
                        dve.wait_ge(s_gate_ps, 1)
                        dve.tensor_copy(gate_t[:, :], front_bank[:, 0:E]).then_inc(s_gate, 1)
                    if h == 10:
                        dve.wait_ge(s_sq, B * (HC + 1))
                        front_h2(0)
                    if h == 12:
                        front_lo(0)
                if not own and h < 3:
                    front_gates(0, h)

            batches(dve, head_step)

            def split_hidden_hi(no, t):
                dve.wait_ge(s_silu, no + 1)
                at_least(dve, s_l2, no - HR + 1)
                dve.tensor_copy(h_hi[t % HR], hidden[:, t % HR, :]).then_inc(s_hhi[0], 1)

            def split_hidden_lo(g, t):
                dve.wait_ge(s_hhi[t % 2], N1 // 2 * g + t // 2 + 1)
                dve.tensor_tensor(h_lo[:, t % HR, :], hidden[:, t % HR, :], h_hi[t % HR].bitcast(F32),
                                  ALU.subtract).then_inc(s_hlo, 1)

            def expert_step(g, own, prev, nxt):
                for t in range(N1):
                    if not prev and t + CLOSING < H:
                        head_step(B, t + CLOSING, False, True, False)
                    if own and t % 2 == 0:
                        split_hidden_hi(N1 * g + t, t)
                    if own and t % 2 == 1:
                        split_hidden_lo(g, t)
                    if (own and t % HC == 1 and t > HC + 1) or (prev and t in (1, HC + 1)):
                        e = (t // HC - 2) % E
                        no = E * g + t // HC - 2
                        dve.wait_ge(s_wide[e // HALF_E], 16 * (g + 1 if t > HC + 1 else g))
                        if e == 0:
                            at_least(dve, s_gated2, g)
                        elif t <= HC + 1:
                            dve.wait_ge(s_sum, (E - 1) * (g - 1) + e - 2)
                        else:
                            at_least(dve, s_sum, (E - 1) * g + max(e - 2, 0))
                        dst = summed if e == 0 else masked[:, e % 2, :]
                        for i, part in parts(own or e < E - 1):
                            dve.wait_ge(s_yout, no + 1 + i)
                            dve.tensor_tensor(dst[:, part], y_out[:, e % 2, part], mask_wide[:, e, part],
                                              ALU.mult).then_inc(s_masked, 1)
                    if prev and t == 12:
                        for i, part in parts(own):
                            dve.wait_ge(s_back, g + i)
                            n = (part.stop - part.start) // D
                            at = bass.ds((g - 1) * GT + i * n, n)
                            dve.tensor_tensor(x_sb[:, at, :], x_sb[:, at, :], bank[5 + i][:, 0:n * D].rearrange(
                                "p (t d) -> p t d", t=n), ALU.add).then_inc(s_final, 1)
                    if nxt and t == 8:
                        front_stats(g + 1)
                    if nxt and t == 10:
                        front_mean_var(g + 1)
                    if nxt and t == 14:
                        front_normed(g + 1)
                    if nxt and t == 18:
                        front_h2(g + 1)
                    if nxt and t == 22:
                        front_lo(g + 1)
                    if nxt and t in (24, 26, 27):
                        front_gates(g + 1, (t - 23) // 2)
                    if own and t % 2 == 0:
                        split_hidden_lo(g, t)

            groups(dve, expert_step)

        @block.scalar
        def _(act):
            act.wait_ge(s_cols, 16)
            act.activation(silu_c[:, 0, :], cols[:, C_C:C_C + B], ACT.Exp, scale=-1.0).then_inc(s_cexp, 1)

            def evacuate_qk(b):
                act.wait_ge(s_qk_ps, b + 1)
                at_least(act, s_lo, 2 * b)
                act.activation(qk[:, 0, :], front_bank[:, 0:S], ACT.Identity, bias=bq_scaled[:, 0:1],
                               scale=SCORE_SCALE).then_inc(s_qk, 1)
                act.activation(qk[:, 1, :], front_bank[:, S:2 * S], ACT.Identity,
                               bias=cols[:, C_BK:C_BK + 1]).then_inc(s_qk, 1)

            def split_hi(b):
                at_least(act, s_rep_ps, QUADS * b)
                act.wait_ge(s_qk, 2 * (b + 1))
                for i in range(2):
                    half_p = slice(i * P // 2, (i + 1) * P // 2)
                    act.activation(qk_parts[half_p, i, :, :], qk[half_p, :, :], ACT.Copy).then_inc(s_hi, 1)

            def evacuate_stack(b, g):
                act.wait_ge(s_rep_ps, QUADS * b + g + 1)
                at_least(act, s_score, H * (b - 1) + HT * (g + 1))
                act.activation(stack[:, g, :, :], stack_bank[g % 2][:, :].rearrange("p (i s) -> p i s", i=2),
                               ACT.Copy).then_inc(s_rep, 1)

            act.wait_ge(s_bq, 1)
            evacuate_qk(0)
            split_hi(0)
            evacuate_stack(0, 0)

            def front_mask(g):
                act.wait_ge(s_mask_ps, g + 1)
                at_least(act, s_mask_out, 16 * g)
                act.activation(mask_t[:, :], front_bank[0:E, :], ACT.Copy).then_inc(s_mask, 1)

            def front_hi(g):
                act.wait_ge(s_h2, g + 1)
                act.activation(x_hi[:, bass.ds(g, 1), :], h2_t[:, :].unsqueeze(1), ACT.Copy).then_inc(s_xhi, 1)

            def head_step(b, h, own, prev, nxt):
                if own and h < QUADS - 2:
                    evacuate_stack(b, h + 1)
                if (own and h >= 3) or (prev and h < 3):
                    n = b * H + h - 3
                    slot = (h - 3) % PR
                    act.wait_ge(s_t, n + 1)
                    if slot % HT == 0:
                        at_least(act, s_pv, b * QUADS + (h - 3) // HT - 1)
                    act.activation(probs[:, slot, :, :],
                                   turned_bank[(h - 3) % 2][:, :].rearrange("p (k q) -> p k q", k=QT),
                                   ACT.Exp, scale=-1.0).then_inc(s_p, 1)
                if (prev and h == 3) or (own and h == 11):
                    pair = b * PAIRS + (h - 3) // 8 - 1
                    act.wait_ge(s_pv, 2 * (pair + 1))
                    at_least(act, s_oT, pair)
                    act.activation(o_sb[:, :], pv_bank[:, 0:S], ACT.Copy).then_inc(s_o, 1)
                if own and h in (5, 6):
                    if h == 5:
                        act.wait_ge(s_exp_w, 32 * (b + 1))
                        at_least(act, s_nrm, b)
                    for k in ((0, 1), (2, 3))[h - 5]:
                        act.activation(squares[:, k * D:(k + 1) * D], w1_raw[:, k, :],
                                       ACT.Square, accum_out=norm_sq[:, k:k + 1]).then_inc(s_sq, 1)
                if own and h == 7:
                    act.wait_ge(s_sq, (HC + 1) * b + HC)
                    act.activation(squares[:, :], w2_raw[:, :], ACT.Square,
                                   accum_out=norm_sq[:, HC:HC + 1]).then_inc(s_sq, 1)
                if own and h == 7:
                    act.wait_ge(s_exp_t, 32 * (b + 1))
                    act.activation(w1_hi[:, bass.ds(b, 1), :], w1_t[:, :].unsqueeze(1), ACT.Copy).then_inc(s_w1h, 1)
                if own and h == 12:
                    act.activation(w2_hi[:, bass.ds(b, 1), :, :], w2_t[:, :, :].unsqueeze(1),
                                   ACT.Copy).then_inc(s_w2h, 1)
                if prev and h == 8:
                    act.wait_ge(s_aT_ps, b)
                    act.activation(attn_t[:, :], tail_bank[:, 0:S], ACT.Identity,
                                   bias=cols[:, C_BV:C_BV + 1]).then_inc(s_aT, 1)
                if prev and h == 10:
                    act.wait_ge(s_y, b)
                    act.wait_ge(s_mod, 12)
                    row = bass.ds(b - 1, 1)
                    act.activation(gated_t[:, :], tail_bank[:, S:2 * S], ACT.Identity, bias=ga_col[:, 1, row],
                                   scale=ga_col[:, 0, row]).then_inc(s_yg, 1)
                if nxt and h == 9:
                    evacuate_qk(b + 1)
                if nxt and h == 10:
                    split_hi(b + 1)
                if nxt and h == 14:
                    evacuate_stack(b + 1, 0)
                if own and not nxt:
                    if h == 11:
                        front_hi(0)
                if not own and h == 2:
                    act.activation(silu_first[:, :], cols[:, 0:1], ACT.Silu)
                if not own and h == 5:
                    front_mask(0)

            batches(act, head_step)

            def expert_step(g, own, prev, nxt):
                for t in range(N1):
                    if not prev and t + CLOSING < H:
                        head_step(B, t + CLOSING, False, True, False)
                    if own:
                        e = t // HC
                        no = N1 * g + t
                        act.wait_ge(s_l1, no + 1)
                        at_least(act, s_hlo, no - HR + 1)
                        act.activation(hidden[:, t % HR, :], bank[t % 2][:, :], ACT.Silu,
                                       bias=cols[:, C_B1 + t:C_B1 + t + 1],
                                       scale=w_scale[:, e, t % HC:t % HC + 1]).then_inc(s_silu, 1)
                        if t % 2 == 1:
                            act.wait_ge(s_silu, no + 1)
                            at_least(act, s_l2, no - HR + 1)
                            act.activation(h_hi[t % HR], hidden[:, t % HR, :], ACT.Copy).then_inc(s_hhi[1], 1)
                    if (own and t % HC == 0 and t > HC) or (prev and t in (0, HC)):
                        e = (t // HC - 2) % E
                        no = E * g + t // HC - 2
                        act.wait_ge(s_l2, HC * (no + 1))
                        at_least(act, s_masked, no - 1)
                        for _, part in parts(own or e < E - 1):
                            act.activation(y_out[:, e % 2, part], bank[2 + e % 2][:, part], ACT.Identity,
                                           bias=cols[:, C_B2 + e:C_B2 + e + 1],
                                           scale=w_scale[:, e, HC:HC + 1]).then_inc(s_yout, 1)
                    if prev and t == 8:
                        for i in range(GB):
                            act.wait_ge(s_sum, (E - 1) * g + (0 if own else i))
                            last = act.activation(gated2[:, i * S:(i + 1) * S], summed[:, i * S:(i + 1) * S],
                                                  ACT.Copy, scale=gb_col[:, bass.ds((g - 1) * GB + i, 1)])
                            if i == GB - 1 or not own:
                                last.then_inc(s_gated2, 1)
                    if nxt and t == 20:
                        front_hi(g + 1)
                    if nxt and t == 30:
                        front_mask(g + 1)

            groups(act, expert_step)

        @block.tensor
        def _(pe):
            def turn(dst, src, n=P):
                return pe.transpose(dst, src, ident[0:n, 0:n])

            def turn_normed(b):
                pe.wait_ge(s_norm, b + 1)
                at_least(pe, s_v, b)
                for qt in range(QT):
                    last = turn(front_bank[:, qt * P:(qt + 1) * P], normed[:, qt, :])
                last.then_inc(s_hT_ps, 1)

            def project_qk(b):
                pe.wait_ge(s_hT, b + 1)
                for i in range(2):
                    last = pe.matmul(front_bank[:, i * S:(i + 1) * S], w_t[:, i, :], h_t[:, :], start=True, stop=True)
                last.then_inc(s_qk_ps, 1)

            def make_stack(b, g):
                pe.wait_ge(s_lo, 2 * (b + 1))
                if g == 1:
                    at_least(pe, s_rep_last, b)
                else:
                    at_least(pe, s_rep, (QUADS - 1) * b + max(g - 1, 0))
                if g == 1:
                    at_least(pe, s_x2, b - 1)
                for i in range(2):
                    choose = sel[:, i, g, :, :, :].rearrange("p j r d -> p (j r d)")
                    last = pe.matmul(stack_bank[g % 2][:, i * S:(i + 1) * S], choose, qk_parts[:, g // 2, i, :],
                                     start=True, stop=True)
                last.then_inc(s_rep_ps, 1)

            pe.wait_ge(s_ident, 1)
            def stay_warm(turns, times):
                for _ in range(turns):
                    last = turn(bank[1][:, 0:P], ident[:, :])
                last.then_inc(s_warm, 1)
                pe.wait_ge(s_warm, times)

            stay_warm(20, 1)
            turn_normed(0)
            pe.wait_ge(s_wmod, 16)
            pe.wait_ge(s_sc, 3)
            for j in range(6):
                half_bank, at = (bank[2], j) if j < 2 else (bank[3], j - 2)
                last = pe.matmul(half_bank[:, at * B:(at + 1) * B], wmod_sb[:, j * D:(j + 1) * D], silu_c[:, 0, :],
                                 start=True, stop=True)
                if j in (1, 5):
                    last.then_inc(s_mod_ps, 1)
            pe.wait_ge(s_w, 16)
            project_qk(0)
            stay_warm(16, 2)
            pe.wait_ge(s_sel, 12)
            for g in range(2):
                make_stack(0, g)

            def front_turn(g):
                pe.wait_ge(s_norm2, g + 1)
                at_least(pe, s_mask, g)
                for t in range(GT):
                    last = turn(front_bank[:, t * P:(t + 1) * P], normed2[:, t, :])
                last.then_inc(s_h2_ps, 1)

            def front_logits(g):
                pe.wait_ge(s_h2, g + 1)
                pe.wait_ge(s_gate, 1)
                for t in range(GT):
                    last = pe.matmul(front_bank[:, t * E:(t + 1) * E], h2_t[:, t * P:(t + 1) * P], gate_t[:, :],
                                     start=True, stop=True)
                last.then_inc(s_logit_ps, 1)

            def front_mask(g):
                pe.wait_ge(s_chosen, 2 * g + 2)
                for t in range(GT):
                    last = turn(front_bank[0:E, t * P:(t + 1) * P], chosen[:, 2, t, :])
                last.then_inc(s_mask_ps, 1)

            def head_step(b, h, own, prev, nxt):
                n = b * H + h
                if own:
                    g, j = h // HT, h % HT
                    if j == 0:
                        if g < QUADS - 1:
                            pe.wait_ge(s_rep, (QUADS - 1) * b + g + 1)
                        else:
                            pe.wait_ge(s_rep_last, b + 1)
                    at_least(pe, s_z, n - 1)
                    for qt in range(QT):
                        part = stack[32 * j:32 * (j + 1), g, :, :]
                        last = pe.matmul(score_bank[h % 2][:, qt * S:(qt + 1) * S],
                                         part[:, 0, qt * P:(qt + 1) * P], part[:, 1, :], start=True, stop=True)
                    last.then_inc(s_score, 1)
                if (own and h >= 3) or (prev and h < 3):
                    m = b * H + h - 3
                    slot = (h - 3) % ZR
                    pe.wait_ge(s_w_sub, m + 1)
                    at_least(pe, s_p, m - 1)
                    for qt in range(QT):
                        for kt in range(QT):
                            at = kt * S + qt * P
                            last = turn(turned_bank[(h - 3) % 2][:, at:at + P],
                                        w[:, slot, qt, kt * P:(kt + 1) * P])
                    last.then_inc(s_t, 1)
                if (prev and h == 3) or (own and h in (7, 11, 15)):
                    quad = b * QUADS + (h - 7) // 4
                    g = ((h - 7) // 4) % QUADS
                    pe.wait_ge(s_p, HT * (quad + 1))
                    if g % 2 == 0:
                        at_least(pe, s_o, b * PAIRS + g // 2)
                    if h == 7:
                        pe.wait_ge(s_v, b + 1)
                    for kt in range(QT):
                        for j in range(HT):
                            last = pe.matmul(pv_bank[32 * j:32 * (j + 1), 0:S], v_wide[:, kt, HT * g + j, :],
                                             probs[:, (HT * g + j) % PR, kt, :],
                                             start=(g % 2 == 0 and kt == 0),
                                             stop=(g % 2 == 1 and kt == QT - 1), skip_group_check=True)
                    last.then_inc(s_pv, 1)
                if (prev and h == 5) or (own and h == 13):
                    pair = b * PAIRS + (h - 5) // 8 - 1
                    pe.wait_ge(s_o, pair + 1)
                    at_least(pe, s_at, pair)
                    for qt in range(QT):
                        last = turn(ot_bank[:, qt * P:(qt + 1) * P], o_sb[:, qt * P:(qt + 1) * P])
                    last.then_inc(s_oT, 1)
                if own and h < 2:
                    make_stack(b, h + 2)
                if own and h == 3:
                    pe.wait_ge(s_rep, (QUADS - 1) * (b + 1))
                    for qt in range(QT):
                        last = pe.matmul(front_bank[:, qt * D:(qt + 1) * D], h_t[:, qt * P:(qt + 1) * P],
                                         w_t[:, 2, :], start=True, stop=True)
                    last.then_inc(s_v_ps, 1)
                if nxt and h == 6:
                    turn_normed(b + 1)
                if prev and h == 8:
                    if own:
                        pe.wait_ge(s_rep_last, b + 1)
                    pe.wait_ge(s_at, PAIRS * b)
                    for qt in range(QT):
                        last = turn(tail_bank[:, qt * P:(qt + 1) * P], attn[:, qt, :])
                    last.then_inc(s_aT_ps, 1)
                if prev and h == 10:
                    pe.wait_ge(s_aT, b)
                    pe.matmul(tail_bank[:, S:2 * S], w_t[:, 3, :], attn_t[:, :], start=True,
                              stop=True).then_inc(s_y, 1)
                if prev and h == 12:
                    pe.wait_ge(s_yg, b)
                    for qt in range(QT):
                        last = turn(tail_bank[:, qt * P:(qt + 1) * P], gated_t[:, qt * P:(qt + 1) * P])
                    last.then_inc(s_yb, 1)
                if nxt and h == 9:
                    project_qk(b + 1)
                if nxt and h >= H - 2:
                    make_stack(b + 1, h - (H - 2))
                if own and not nxt:
                    if h == 6:
                        pe.wait_ge(s_gsq, 4)
                        pe.wait_ge(s_v, B)
                        turn(front_bank[:, 0:E], gate_scaled[:, :], E).then_inc(s_gate_ps, 1)
                    if h == 9:
                        pe.wait_ge(s_gate, 1)
                        front_turn(0)
                    if h == 12:
                        front_logits(0)
                if not own and h == 4:
                    front_mask(0)

            batches(pe, head_step)

            def first_product(g, t):
                e, k = t // HC, t % HC
                no = N1 * g + t
                if t == 0:
                    pe.wait_ge(s_xlo, g + 1)
                at_least(pe, s_silu, no - 1)
                part = slice(k * P, (k + 1) * P)
                for i, (weights, tokens) in enumerate(((w1_hi, x_hi), (w1_hi, x_lo), (w1_lo, x_hi))):
                    last = pe.matmul(bank[t % 2][:, :], weights[:, e, part], tokens[:, bass.ds(g, 1), :],
                                     start=(i == 0), stop=(i == 2))
                last.then_inc(s_l1, 1)

            def second_product(g, t):
                e, k = t // HC, t % HC
                if k == 0:
                    at_least(pe, s_yout, E * g + e - 1)
                pe.wait_ge(s_hlo, N1 * g + t + 1)
                hi, lo = h_hi[t % HR], h_lo[:, t % HR, :]
                for i, (weights, part) in enumerate(((w2_hi, hi), (w2_hi, lo), (w2_lo, hi))):
                    last = pe.matmul(bank[2 + e % 2][:, :], weights[:, e, k, :], part,
                                     start=(k == 0 and i == 0), stop=(k == HC - 1 and i == 2))
                last.then_inc(s_l2, 1)

            def expert_step(g, own, prev, nxt):
                for t in range(N1):
                    if own:
                        first_product(g, t)
                    if not prev and t + CLOSING < H:
                        head_step(B, t + CLOSING, False, True, False)
                    if own and t >= LAG:
                        second_product(g, t - LAG)
                    if prev and t < LAG:
                        second_product(g - 1, N1 + t - LAG)
                    if prev and t == 10:
                        for i, part in parts(own):
                            pe.wait_ge(s_gated2, g + i)
                            for at in range(part.start, part.stop, P):
                                last = turn(bank[5 + i][:, at - part.start:at - part.start + P], gated2[:, at:at + P])
                            last.then_inc(s_back, 1)
                    if nxt and t == 16:
                        front_turn(g + 1)
                    if nxt and t == 21:
                        front_logits(g + 1)
                    if nxt and t == 29:
                        front_mask(g + 1)

            groups(pe, expert_step)


_ATTENTION = ('L0_attn_Wq', 'L0_attn_Wk', 'L0_attn_Wv', 'L0_attn_Wo')
_COLUMNS = {"c": 'L0_c', "bq": 'L0_attn_bq', "bk": 'L0_attn_bk', "bv": 'L0_attn_bv', "bo": 'L0_attn_bo',
            "b1": 'L0_ffn_b1', "w1_g": 'L0_ffn_w1_g', "w2_g": 'L0_ffn_w2_g', "b2": 'L0_ffn_b2'}


def kernel(**inputs):
    import numpy as _np
    import concourse.bacc as _bacc
    from concourse import mybir as _mybir
    from concourse.bass_utils import run_bass_kernel_spmd as _run

    nc = _bacc.Bacc("TRN2", target_bir_lowering=False, num_devices=1)
    D = inputs['L0_attn_x'].shape[2]
    rel = inputs['L0_attn_rel_bias']
    S = inputs['L0_attn_x'].shape[1]
    reach = (rel.shape[1] - 1) // 2
    at = _np.clip(_np.arange(2 * S) - (S - 1), -reach, reach) + reach
    E, HID = inputs['L0_ffn_b1'].shape
    places, _ = column_places(inputs['L0_c'].shape[0], E, HID // P)
    columns = _np.concatenate([inputs[_COLUMNS[name]].reshape(-1, D) for name in places], axis=0).T
    ins = {
        "x": inputs['L0_attn_x'],
        "w_in_out": _np.stack([inputs[name].T for name in _ATTENTION], axis=1),
        "columns": columns,
        "rel_ext": rel[:, at],
        "gate_v": inputs['L0_ffn_gate_v'], "gate_g": inputs['L0_ffn_gate_g'], "gate_b": inputs['L0_ffn_gate_b'],
        "w1_v": inputs['L0_ffn_w1_v'], "w1_in_hid": inputs['L0_ffn_w1_v'].transpose(0, 2, 1),
        "w2_v": inputs['L0_ffn_w2_v'], "w2_hid_out": inputs['L0_ffn_w2_v'].transpose(0, 2, 1),
        "wmod": inputs['L0_wmod'],
    }
    arrays, args = {}, []
    for name, a in ins.items():
        a = _np.ascontiguousarray(a)
        arrays[f"in_{name}_dram"] = a
        args.append(nc.dram_tensor(f"in_{name}_dram", a.shape, _mybir.dt.from_np(a.dtype), kind="ExternalInput").ap())
    out = nc.dram_tensor("out_0_dram", inputs['L0_attn_x'].shape, _mybir.dt.float32, kind="ExternalOutput").ap()
    adaln_block_kernel(nc, *args, out)
    r = _run(nc, [arrays], core_ids=[0])
    return r.results[0]["out_0_dram"]
```
